# Optimizing a Trainium2 kernel written in Bass

```python
import numpy as np
import jax
import jax.numpy as jnp

def _softmax(x, axis=-1):
    return jax.nn.softmax(x, axis=axis)

def _gelu(x):
    return jax.nn.gelu(x, approximate=True)

def _silu(x):
    return jax.nn.silu(x)

def _sigmoid(x):
    return jax.nn.sigmoid(x)

def _layernorm(x, axis=-1, eps=1e-05):
    m = jnp.mean(x, axis=axis, keepdims=True)
    v = jnp.var(x, axis=axis, keepdims=True)
    return (x - m) / jnp.sqrt(v + eps)

def _scatter_add(tgt, idx, src, axis=0):
    return tgt.at[idx].add(src)

def _segment_sum(src, seg, n):
    return jax.ops.segment_sum(src, seg, n)
kernel_name = 'mk_pixart_seq_d2_seqx_r8_bcbde1'

def setup_inputs(seed: int=0):
    np.random.seed(seed)
    _w = jnp.asarray

    def _rec_inputs():
        import jax
        import jax.numpy as jnp
        _rk = jax.random.key(seed)
        x = -0.0002928 + 1 * jax.random.normal(jax.random.fold_in(_rk, 1), (16, 64, 128), jnp.float32)
        _lenS = 64 - jax.random.randint(jax.random.fold_in(_rk, 7), (16,), 0, max(1, 64 // 4) + 1, jnp.int32)
        _lenS2 = 64 - jax.random.randint(jax.random.fold_in(_rk, 8), (16,), 0, max(1, 64 // 4) + 1, jnp.int32)
        cond_1024 = 0.000887014 + 1.03683 * jax.random.normal(jax.random.fold_in(_rk, 11), (16, 128), jnp.float32)
        _ctx_1024P = jax.random.normal(jax.random.fold_in(_rk, 12), (16, 16, 128), jnp.float32)
        _ctx_1024c = jax.random.dirichlet(jax.random.fold_in(_rk, 512), 0.3 * jnp.ones((16,), jnp.float32), (16, 64))
        _ctx_1024t = jnp.einsum('bsk,bkd->bsd', _ctx_1024c, _ctx_1024P)
        _ctx_1024t = _ctx_1024t * jax.lax.rsqrt(jnp.mean(jnp.square(_ctx_1024t)) + 1e-12) * 0.953939
        ctx_1024 = 0.00086875 + 0.999764 * (_ctx_1024t + 0.3 * jax.random.normal(jax.random.fold_in(_rk, 612), (16, 64, 128), jnp.float32))
        return (x, cond_1024, ctx_1024)
    x, cond_1024, ctx_1024 = _rec_inputs()

    def _L0_xcond_setup():
        import jax, jax.numpy as jnp
        import numpy as np
        import math
        D_MODEL = 128
        N_HEADS = 16
        HEAD_DIM = D_MODEL // N_HEADS
        D_FF = 512
        EPS = 1e-05
        ROPE_BASE = 10000.0

        def _rope(t):
            L, Dh = (t.shape[1], t.shape[-1])
            half = Dh // 2
            inv_freq = 1.0 / ROPE_BASE ** (jnp.arange(half, dtype=t.dtype) / half)
            ang = jnp.arange(L, dtype=t.dtype)[:, None] * inv_freq[None, :]
            cos = jnp.cos(ang)[None, :, None, :]
            sin = jnp.sin(ang)[None, :, None, :]
            t1, t2 = (t[..., :half], t[..., half:])
            return jnp.concatenate([t1 * cos - t2 * sin, t2 * cos + t1 * sin], axis=-1)

        def _adaln(x, emb, w, b):
            e = emb[:, 0, :]
            gb = e @ w.T + b
            gamma, beta = jnp.split(gb, 2, axis=-1)
            mu = x.mean(-1, keepdims=True)
            var = x.var(-1, keepdims=True)
            xn = (x - mu) * jax.lax.rsqrt(var + EPS)
            return xn * (1.0 + gamma[:, None, :]) + beta[:, None, :]

        def _attn(q, k, v):
            scale = 1.0 / math.sqrt(HEAD_DIM)
            scores = jnp.einsum('bqhd,bkhd->bhqk', q, k) * scale
            w = jax.nn.softmax(scores, axis=-1)
            out = jnp.einsum('bhqk,bkhd->bqhd', w, v)
            B, Lq = (out.shape[0], out.shape[1])
            return out.reshape(B, Lq, D_MODEL)
        key = jax.random.key(seed)
        ks = jax.random.split(key, 24)
        s = 0.02
        inp = {'x': jax.random.normal(ks[0], (2, 256, D_MODEL), jnp.float32), 'noise_emb': jax.random.normal(ks[1], (2, 1, D_MODEL), jnp.float32), 'context': jax.random.normal(ks[2], (2, 128, D_MODEL), jnp.float32), 'ln1_w': jax.random.normal(ks[3], (2 * D_MODEL, D_MODEL), jnp.float32) * s, 'ln1_b': jax.random.normal(ks[4], (2 * D_MODEL,), jnp.float32) * s, 'ln2_w': jax.random.normal(ks[5], (2 * D_MODEL, D_MODEL), jnp.float32) * s, 'ln2_b': jax.random.normal(ks[6], (2 * D_MODEL,), jnp.float32) * s, 'ln3_w': jax.random.normal(ks[7], (2 * D_MODEL, D_MODEL), jnp.float32) * s, 'ln3_b': jax.random.normal(ks[8], (2 * D_MODEL,), jnp.float32) * s, 'qkv_w': jax.random.normal(ks[9], (3 * D_MODEL, D_MODEL), jnp.float32) * s, 'sa_out_w': jax.random.normal(ks[10], (D_MODEL, D_MODEL), jnp.float32) * s, 'q_w': jax.random.normal(ks[11], (D_MODEL, D_MODEL), jnp.float32) * s, 'k_w': jax.random.normal(ks[12], (D_MODEL, D_MODEL), jnp.float32) * s, 'v_w': jax.random.normal(ks[13], (D_MODEL, D_MODEL), jnp.float32) * s, 'ca_out_w': jax.random.normal(ks[14], (D_MODEL, D_MODEL), jnp.float32) * s, 'ffn_w1': jax.random.normal(ks[15], (D_FF, D_MODEL), jnp.float32) * s, 'ffn_b1': jax.random.normal(ks[16], (D_FF,), jnp.float32) * s, 'ffn_w2': jax.random.normal(ks[17], (D_MODEL, D_FF), jnp.float32) * s, 'ffn_b2': jax.random.normal(ks[18], (D_MODEL,), jnp.float32) * s}
        return inp
    _L0_xcond_all = _L0_xcond_setup()
    _L0_xcond_in = {k: v for k, v in _L0_xcond_all.items() if k in ('ln1_w', 'ln1_b', 'ln2_w', 'ln2_b', 'ln3_w', 'ln3_b', 'qkv_w', 'sa_out_w', 'q_w', 'k_w', 'v_w', 'ca_out_w', 'ffn_w1', 'ffn_b1', 'ffn_w2', 'ffn_b2')}
    del _L0_xcond_all

    def _L1_xcond_setup():
        import jax, jax.numpy as jnp
        import numpy as np
        LN_EPS = 1e-06

        def _ln(x):
            mu = jnp.mean(x, axis=-1, keepdims=True)
            var = jnp.var(x, axis=-1, keepdims=True)
            return (x - mu) * jax.lax.rsqrt(var + LN_EPS)
        key = jax.random.key(seed)
        H, NH = (128, 16)
        B, N, S = (4, 128, 77)
        MLP = int(H * 4.0)
        ks = jax.random.split(key, 20)
        s = 1.0 / np.sqrt(H)
        return {'x': jax.random.normal(ks[0], (B, N, H), jnp.float32), 'c': jax.random.normal(ks[1], (B, H), jnp.float32), 'context': jax.random.normal(ks[2], (B, S, H), jnp.float32), 'W_mod': jax.random.normal(ks[3], (H, 6 * H), jnp.float32) * s, 'b_mod': jnp.zeros((6 * H,), jnp.float32), 'W_qkv': jax.random.normal(ks[4], (H, 3 * H), jnp.float32) * s, 'b_qkv': jnp.zeros((3 * H,), jnp.float32), 'W_proj': jax.random.normal(ks[5], (H, H), jnp.float32) * s, 'b_proj': jnp.zeros((H,), jnp.float32), 'W_qc': jax.random.normal(ks[6], (H, H), jnp.float32) * s, 'b_qc': jnp.zeros((H,), jnp.float32), 'W_kvc': jax.random.normal(ks[7], (H, 2 * H), jnp.float32) * s, 'b_kvc': jnp.zeros((2 * H,), jnp.float32), 'W_cproj': jax.random.normal(ks[8], (H, H), jnp.float32) * s, 'b_cproj': jnp.zeros((H,), jnp.float32), 'W_mlp1': jax.random.normal(ks[9], (H, MLP), jnp.float32) * s, 'b_mlp1': jnp.zeros((MLP,), jnp.float32), 'W_mlp2': jax.random.normal(ks[10], (MLP, H), jnp.float32) * (1.0 / np.sqrt(MLP)), 'b_mlp2': jnp.zeros((H,), jnp.float32)}
    _L1_xcond_all = _L1_xcond_setup()
    _L1_xcond_in = {k: v for k, v in _L1_xcond_all.items() if k in ('W_mod', 'b_mod', 'W_qkv', 'b_qkv', 'W_proj', 'b_proj', 'W_qc', 'b_qc', 'W_kvc', 'b_kvc', 'W_cproj', 'b_cproj', 'W_mlp1', 'b_mlp1', 'W_mlp2', 'b_mlp2')}
    del _L1_xcond_all
    return {'x': x, 'cond_1024': cond_1024, 'ctx_1024': ctx_1024, 'L0_xcond_ln1_w': _L0_xcond_in['ln1_w'], 'L0_xcond_ln1_b': _L0_xcond_in['ln1_b'], 'L0_xcond_ln2_w': _L0_xcond_in['ln2_w'], 'L0_xcond_ln2_b': _L0_xcond_in['ln2_b'], 'L0_xcond_ln3_w': _L0_xcond_in['ln3_w'], 'L0_xcond_ln3_b': _L0_xcond_in['ln3_b'], 'L0_xcond_qkv_w': _L0_xcond_in['qkv_w'], 'L0_xcond_sa_out_w': _L0_xcond_in['sa_out_w'], 'L0_xcond_q_w': _L0_xcond_in['q_w'], 'L0_xcond_k_w': _L0_xcond_in['k_w'], 'L0_xcond_v_w': _L0_xcond_in['v_w'], 'L0_xcond_ca_out_w': _L0_xcond_in['ca_out_w'], 'L0_xcond_ffn_w1': _L0_xcond_in['ffn_w1'], 'L0_xcond_ffn_b1': _L0_xcond_in['ffn_b1'], 'L0_xcond_ffn_w2': _L0_xcond_in['ffn_w2'], 'L0_xcond_ffn_b2': _L0_xcond_in['ffn_b2'], 'L1_xcond_W_mod': _L1_xcond_in['W_mod'], 'L1_xcond_b_mod': _L1_xcond_in['b_mod'], 'L1_xcond_W_qkv': _L1_xcond_in['W_qkv'], 'L1_xcond_b_qkv': _L1_xcond_in['b_qkv'], 'L1_xcond_W_proj': _L1_xcond_in['W_proj'], 'L1_xcond_b_proj': _L1_xcond_in['b_proj'], 'L1_xcond_W_qc': _L1_xcond_in['W_qc'], 'L1_xcond_b_qc': _L1_xcond_in['b_qc'], 'L1_xcond_W_kvc': _L1_xcond_in['W_kvc'], 'L1_xcond_b_kvc': _L1_xcond_in['b_kvc'], 'L1_xcond_W_cproj': _L1_xcond_in['W_cproj'], 'L1_xcond_b_cproj': _L1_xcond_in['b_cproj'], 'L1_xcond_W_mlp1': _L1_xcond_in['W_mlp1'], 'L1_xcond_b_mlp1': _L1_xcond_in['b_mlp1'], 'L1_xcond_W_mlp2': _L1_xcond_in['W_mlp2'], 'L1_xcond_b_mlp2': _L1_xcond_in['b_mlp2']}

def reference(x, cond_1024, ctx_1024, L0_xcond_ln1_w, L0_xcond_ln1_b, L0_xcond_ln2_w, L0_xcond_ln2_b, L0_xcond_ln3_w, L0_xcond_ln3_b, L0_xcond_qkv_w, L0_xcond_sa_out_w, L0_xcond_q_w, L0_xcond_k_w, L0_xcond_v_w, L0_xcond_ca_out_w, L0_xcond_ffn_w1, L0_xcond_ffn_b1, L0_xcond_ffn_w2, L0_xcond_ffn_b2, L1_xcond_W_mod, L1_xcond_b_mod, L1_xcond_W_qkv, L1_xcond_b_qkv, L1_xcond_W_proj, L1_xcond_b_proj, L1_xcond_W_qc, L1_xcond_b_qc, L1_xcond_W_kvc, L1_xcond_b_kvc, L1_xcond_W_cproj, L1_xcond_b_cproj, L1_xcond_W_mlp1, L1_xcond_b_mlp1, L1_xcond_W_mlp2, L1_xcond_b_mlp2):
    import jax
    import jax.numpy as jnp

    def _L0_xcond_ref(x, noise_emb, context, ln1_w, ln1_b, ln2_w, ln2_b, ln3_w, ln3_b, qkv_w, sa_out_w, q_w, k_w, v_w, ca_out_w, ffn_w1, ffn_b1, ffn_w2, ffn_b2):
        import jax, jax.numpy as jnp
        import numpy as np
        import math
        D_MODEL = 128
        N_HEADS = 16
        HEAD_DIM = D_MODEL // N_HEADS
        D_FF = 512
        EPS = 1e-05
        ROPE_BASE = 10000.0

        def _rope(t):
            L, Dh = (t.shape[1], t.shape[-1])
            half = Dh // 2
            inv_freq = 1.0 / ROPE_BASE ** (jnp.arange(half, dtype=t.dtype) / half)
            ang = jnp.arange(L, dtype=t.dtype)[:, None] * inv_freq[None, :]
            cos = jnp.cos(ang)[None, :, None, :]
            sin = jnp.sin(ang)[None, :, None, :]
            t1, t2 = (t[..., :half], t[..., half:])
            return jnp.concatenate([t1 * cos - t2 * sin, t2 * cos + t1 * sin], axis=-1)

        def _adaln(x, emb, w, b):
            e = emb[:, 0, :]
            gb = e @ w.T + b
            gamma, beta = jnp.split(gb, 2, axis=-1)
            mu = x.mean(-1, keepdims=True)
            var = x.var(-1, keepdims=True)
            xn = (x - mu) * jax.lax.rsqrt(var + EPS)
            return xn * (1.0 + gamma[:, None, :]) + beta[:, None, :]

        def _attn(q, k, v):
            scale = 1.0 / math.sqrt(HEAD_DIM)
            scores = jnp.einsum('bqhd,bkhd->bhqk', q, k) * scale
            w = jax.nn.softmax(scores, axis=-1)
            out = jnp.einsum('bhqk,bkhd->bqhd', w, v)
            B, Lq = (out.shape[0], out.shape[1])
            return out.reshape(B, Lq, D_MODEL)
        B, L, D = x.shape
        L_ctx = context.shape[1]
        res = x
        xn = _adaln(x, noise_emb, ln1_w, ln1_b)
        qkv = xn @ qkv_w.T
        q, k, v = jnp.split(qkv, 3, axis=-1)
        q = _rope(q.reshape(B, L, N_HEADS, HEAD_DIM))
        k = _rope(k.reshape(B, L, N_HEADS, HEAD_DIM))
        v = v.reshape(B, L, N_HEADS, HEAD_DIM)
        sa = _attn(q, k, v) @ sa_out_w.T
        x = res + sa
        res = x
        xn = _adaln(x, noise_emb, ln2_w, ln2_b)
        q = _rope((xn @ q_w.T).reshape(B, L, N_HEADS, HEAD_DIM))
        k = _rope((context @ k_w.T).reshape(B, L_ctx, N_HEADS, HEAD_DIM))
        v = (context @ v_w.T).reshape(B, L_ctx, N_HEADS, HEAD_DIM)
        ca = _attn(q, k, v) @ ca_out_w.T
        x = res + ca
        res = x
        xn = _adaln(x, noise_emb, ln3_w, ln3_b)
        h = jax.nn.gelu(xn @ ffn_w1.T + ffn_b1, approximate=False)
        x = res + (h @ ffn_w2.T + ffn_b2)
        return x

    def _L1_xcond_ref(x, c, context, W_mod, b_mod, W_qkv, b_qkv, W_proj, b_proj, W_qc, b_qc, W_kvc, b_kvc, W_cproj, b_cproj, W_mlp1, b_mlp1, W_mlp2, b_mlp2):
        import jax, jax.numpy as jnp
        import numpy as np
        LN_EPS = 1e-06

        def _ln(x):
            mu = jnp.mean(x, axis=-1, keepdims=True)
            var = jnp.var(x, axis=-1, keepdims=True)
            return (x - mu) * jax.lax.rsqrt(var + LN_EPS)
        B, N, H = x.shape
        NH = 16
        hd = H // NH
        scale = hd ** (-0.5)
        c_proj = jax.nn.silu(c) @ W_mod + b_mod
        shift_a, scale_a, gate_a, shift_m, scale_m, gate_m = jnp.split(c_proj, 6, axis=-1)

        def modulate(t, shift, sc):
            return t * (1 + sc[:, None]) + shift[:, None]
        x_norm = modulate(_ln(x), shift_a, scale_a)
        qkv = x_norm @ W_qkv + b_qkv
        q, k, v = jnp.split(qkv, 3, axis=-1)
        q = q.reshape(B, N, NH, hd).transpose(0, 2, 1, 3)
        k = k.reshape(B, N, NH, hd).transpose(0, 2, 1, 3)
        v = v.reshape(B, N, NH, hd).transpose(0, 2, 1, 3)
        attn_w = jax.nn.softmax(jnp.einsum('bhqd,bhkd->bhqk', q, k) * scale, axis=-1)
        attn_out = jnp.einsum('bhqk,bhkd->bhqd', attn_w, v)
        attn_out = attn_out.transpose(0, 2, 1, 3).reshape(B, N, H)
        attn_out = attn_out @ W_proj + b_proj
        x = x + gate_a[:, None] * attn_out
        S = context.shape[1]
        q_c = _ln(x) @ W_qc + b_qc
        kv_c = _ln(context) @ W_kvc + b_kvc
        k_c, v_c = jnp.split(kv_c, 2, axis=-1)
        q_c = q_c.reshape(B, N, NH, hd).transpose(0, 2, 1, 3)
        k_c = k_c.reshape(B, S, NH, hd).transpose(0, 2, 1, 3)
        v_c = v_c.reshape(B, S, NH, hd).transpose(0, 2, 1, 3)
        c_attn_w = jax.nn.softmax(jnp.einsum('bhqd,bhsd->bhqs', q_c, k_c) * scale, axis=-1)
        c_attn_out = jnp.einsum('bhqs,bhsd->bhqd', c_attn_w, v_c)
        c_attn_out = c_attn_out.transpose(0, 2, 1, 3).reshape(B, N, H)
        c_attn_out = c_attn_out @ W_cproj + b_cproj
        x = x + c_attn_out
        x_norm2 = modulate(_ln(x), shift_m, scale_m)
        h = jax.nn.gelu(x_norm2 @ W_mlp1 + b_mlp1)
        h = h @ W_mlp2 + b_mlp2
        x = x + gate_m[:, None] * h
        return x
    x = _L0_xcond_ref(x, cond_1024[:, None, :], ctx_1024, L0_xcond_ln1_w, L0_xcond_ln1_b, L0_xcond_ln2_w, L0_xcond_ln2_b, L0_xcond_ln3_w, L0_xcond_ln3_b, L0_xcond_qkv_w, L0_xcond_sa_out_w, L0_xcond_q_w, L0_xcond_k_w, L0_xcond_v_w, L0_xcond_ca_out_w, L0_xcond_ffn_w1, L0_xcond_ffn_b1, L0_xcond_ffn_w2, L0_xcond_ffn_b2)
    x = _L1_xcond_ref(x, cond_1024, ctx_1024, L1_xcond_W_mod, L1_xcond_b_mod, L1_xcond_W_qkv, L1_xcond_b_qkv, L1_xcond_W_proj, L1_xcond_b_proj, L1_xcond_W_qc, L1_xcond_b_qc, L1_xcond_W_kvc, L1_xcond_b_kvc, L1_xcond_W_cproj, L1_xcond_b_cproj, L1_xcond_W_mlp1, L1_xcond_b_mlp1, L1_xcond_W_mlp2, L1_xcond_b_mlp2)
    return x

_drawn_inputs = setup_inputs


def setup_inputs(seed=0):
    import zlib

    import numpy as np

    out = dict(_drawn_inputs(seed))
    spreads = {'L1_xcond_b_mod': (0.0, 0.1),
     'L1_xcond_b_qkv': (0.0, 0.1),
     'L1_xcond_b_proj': (0.0, 0.1),
     'L1_xcond_b_qc': (0.0, 0.472),
     'L1_xcond_b_kvc': (0.0, 0.1),
     'L1_xcond_b_cproj': (0.0, 0.1),
     'L1_xcond_b_mlp1': (0.0, 0.362),
     'L1_xcond_b_mlp2': (0.0, 0.1)}
    factors = {'L0_xcond_ln1_w': 4.836,
     'L0_xcond_ln1_b': 8.0,
     'L0_xcond_ln2_w': 8.0,
     'L0_xcond_ln2_b': 64.0,
     'L0_xcond_ln3_w': 3.356,
     'L0_xcond_ln3_b': 63.883,
     'L0_xcond_qkv_w': 4.196,
     'L0_xcond_sa_out_w': 4.185,
     'L0_xcond_q_w': 8.0,
     'L0_xcond_k_w': 8.0,
     'L0_xcond_ffn_b1': 8.0,
     'L0_xcond_ffn_b2': 2.906}
    for name, (base, spread) in spreads.items():
        noise = np.random.default_rng([zlib.crc32(name.encode()), seed]).standard_normal(out[name].shape)
        drawn = base * np.exp(spread * noise) if base else spread * noise
        out[name] = jnp.asarray(drawn.astype(out[name].dtype))
    for name, factor in factors.items():
        out[name] = (out[name] * factor).astype(out[name].dtype)
    return out
```

```python
from contextlib import ExitStack

import numpy as np

import concourse.bass as bass
from concourse import mybir

F32 = mybir.dt.float32
F32R = mybir.dt.float32r
ALU = mybir.AluOpType
ACT = mybir.ActivationFunctionType
AX = mybir.AxisListType

B, S, D = 16, 64, 128
H, HD = 16, 8
FF = 512
PAIRS = B // 2
FFC = FF // 128
SCALE = HD ** -0.5
EPS = {0: 1e-5, 1: 1e-6}

SELF0, CROSS0, FFN0, SELF1, CROSS1, FFN1 = range(6)
KINDS = [SELF0, CROSS0, FFN0, SELF1, CROSS1, FFN1]
LAYER = {SELF0: 0, CROSS0: 0, FFN0: 0, SELF1: 1, CROSS1: 1, FFN1: 1}
ATTN = (SELF0, CROSS0, SELF1, CROSS1)
ROPE = (SELF0, CROSS0)
N_ITEMS = len(KINDS) * PAIRS
LAST_LAG = 5

W_COLS = {}


def _w_columns():
    at = 0
    for name, n in (("q0", 128), ("k0", 128), ("qs0", 128), ("ks0", 128), ("v0", 128), ("o0", 128),
                    ("q1", 128), ("k1", 128), ("qs1", 128), ("ks1", 128), ("v1", 128), ("o1", 128),
                    ("w1_2", FF), ("w2_2", FF),
                    ("q3", 128), ("k3", 128), ("v3", 128), ("o3", 128),
                    ("q4", 128), ("k4", 128), ("v4", 128), ("o4", 128),
                    ("w1_5", FF), ("w2_5", FF)):
        W_COLS[name] = (at, at + n)
        at += n
    return at


W_N = _w_columns()
W_PARTS = [(0, W_COLS["o0"][1]), (W_COLS["q1"][0], W_COLS["o1"][1]), (W_COLS["w1_2"][0], W_COLS["w2_2"][1]),
           (W_COLS["q3"][0], W_COLS["o3"][1]), (W_COLS["q4"][0], W_COLS["o4"][1]),
           (W_COLS["w1_5"][0], W_COLS["w2_5"][1])]

V_LN = 0
V_MOD = 6
V_FB1 = 12
V_MB1 = 16
V_Q3, V_K3, V_Q4, V_K4 = 20, 21, 22, 23
V_BV3, V_BV4 = 24, 25
V_N = 26
R_FB2, R_BP, R_BC, R_MB2, R_GA, R_GM, R_N = 0, 128, 256, 384, 512, 640, 768

C_ID, C_COS, C_SIN, C_HP = 0, 128, 192, 256
C_NEG, C_SEL, C_REP, C_PAIR, C_ONES = 264, 268, 524, 588, 1612
C_DEN, C_HALF, C_N = 1740, 1804, 1806


def _constants():
    c = np.zeros((128, C_N), np.float32)
    c[:, C_ID:C_ID + 128] = np.eye(128, dtype=np.float32)
    half = HD // 2
    inv_freq = (np.float32(1.0) / np.power(np.float32(10000.0), np.arange(half, dtype=np.float32) / half)).astype(np.float32)
    ang = np.arange(S, dtype=np.float32)[:, None] * inv_freq[None, :]
    p = np.arange(128)
    c[:, C_COS:C_COS + S] = np.cos(ang).astype(np.float32).T[p % half]
    sign = np.where(p % HD < half, np.float32(-1), np.float32(1))[:, None]
    c[:, C_SIN:C_SIN + S] = sign * np.sin(ang).astype(np.float32).T[p % half]
    c[p, C_HP + (p // HD) % 8] = 1.0
    for b in range(2):
        for j in range(4):
            for h2 in range(2):
                r = b * 8 + j * 2 + h2
                c[r, C_NEG + j] = -1.0
                c[r, C_SEL + b * 128 + h2 * 64:C_SEL + b * 128 + h2 * 64 + 64] = 1.0
    for r in range(8):
        c[r, C_REP + 8 * r:C_REP + 8 * r + 8] = 1.0
    for b in range(B):
        c[b, C_PAIR + b * S:C_PAIR + (b + 1) * S] = 1.0
    c[:, C_ONES:C_ONES + 128] = 1.0
    for hp in range(8):
        c[:64, C_DEN + hp * 8 + hp % 4] = 1.0
        c[64:, C_DEN + hp * 8 + 4 + hp % 4] = 1.0
    c[:64, C_HALF] = c[64:, C_HALF + 1] = 1.0
    return c


def attention_index(g):
    block, pair = divmod(g, PAIRS)
    return sum(k in ATTN for k in KINDS[:block]) * PAIRS + (pair if KINDS[block] in ATTN else 0)


def ffn_index(g):
    block, pair = divmod(g, PAIRS)
    return sum(k not in ATTN for k in KINDS[:block]) * PAIRS + (pair if KINDS[block] not in ATTN else 0)


def plain_index(g):
    block, pair = divmod(g, PAIRS)
    return sum(k in (SELF1, CROSS1) for k in KINDS[:block]) * PAIRS + (pair if KINDS[block] in (SELF1, CROSS1) else 0)


def rope_index(g):
    block, pair = divmod(g, PAIRS)
    return sum(k in ROPE for k in KINDS[:block]) * PAIRS + (pair if KINDS[block] in ROPE else 0)


ATTN_ITEMS = [g for g in range(N_ITEMS) if KINDS[g // PAIRS] in ATTN]
FFN_ITEMS = [g for g in range(N_ITEMS) if KINDS[g // PAIRS] not in ATTN]


def build(nc, x_d, ctx_d, ctxT_d, condT_d, w_d, lnw_d, wmod_d, vec_d, row_d, const_d, out_d):
    with ExitStack() as stack:
        def sb(name, shape, dt=F32):
            return stack.enter_context(nc.sbuf_tensor(name, shape, dt))

        def ps(name, shape):
            return stack.enter_context(nc.psum_tensor(name, shape, F32))

        def sem(name):
            return stack.enter_context(nc.semaphore(name))

        x = sb("x", [128, PAIRS, D])
        ctx = sb("ctx", [128, PAIRS, D])
        ctxT = sb("ctxT", [D, PAIRS, 2, S])
        w = sb("w", [128, W_N])
        wmod = sb("wmod", [D, 6 * D])
        ln_w = sb("ln_w", [D, 6 * D])
        vec = sb("vec", [D, V_N])
        row = sb("row", [1, R_N])
        const = sb("const", [128, C_N])
        condT = sb("condT", [D, B])
        sel = sb("sel", [16, 2, 128], F32R)
        mod_scale = sb("mod_scale", [D, 5, B])
        mod_shift = sb("mod_shift", [D, 5, B])
        siluT = sb("siluT", [D, B])
        gate = sb("gate", [B, 2 * D])
        gate_rep = sb("gate_rep", [128, PAIRS, 2, D])
        brow = sb("brow", [1, 2, D])
        stats = sb("stats", [128, 2, 2, 6])
        mv = sb("mv", [128, 2, 2, 2])
        var = sb("var", [128, 2, 2])
        rstd = sb("rstd", [128, 2, 2])
        minus_half = sb("minus_half", [128, 1])
        z = sb("z", [128, 2, 2, D])
        xnT = sb("xnT", [D, 3, 2, 2, S])
        t1 = sb("t1", [128, 2, 2, 2, S])
        t2 = sb("t2", [128, 2, 2, 2, S])
        qkT = sb("qkT", [128, 2, 2, 2, S])
        QM = sb("QM", [128, 3, 2, 8, S])
        K2 = sb("K2", [128, 3, 2, 2, S])
        VM = sb("VM", [128, 4, 2, 8, 72])
        m = sb("m", [128, 2, 16])
        mexp = sb("mexp", [16, 2, 4, 128], F32R)
        P = sb("P", [128, 2, 2, 8, S])
        rden = sb("rden", [8, 2, 256])
        rep_sb = sb("rep_sb", [64, 2, 256])
        oT = sb("oT", [128, 2, 2, S])
        hT = sb("hT", [128, 3, FFC, 128])
        gy = sb("gy", [128, 2, D])
        T_ps = ps("T_ps", [128, 512])
        QK_ps = ps("QK_ps", [128, 512])
        VY_ps = ps("VY_ps", [128, 512])
        O_ps = ps("O_ps", [128, 512])
        S_ps = ps("S_ps", [128, 1024])
        ST_ps = ps("ST_ps", [128, 1024])

        ident = const[:, C_ID:C_ID + 128]

        loaded = {n: sem(f"loaded_{n}") for n in ("x", "ctx", "ctxT", "const", "vec", "mod", "row")}
        w_loaded = [sem(f"w_loaded_{n}") for n in range(len(W_PARTS))]
        zeroed = sem("zeroed")
        den_set = sem("den_set")
        silu_done = sem("silu_done")
        mod_ps_done = sem("mod_ps_done")
        mod_ready = sem("mod_ready")
        rows_ps_done = sem("rows_ps_done")
        rows_ready = sem("rows_ready")
        gate_ps_done = sem("gate_ps_done")
        gate_ready = sem("gate_ready")
        sel_ready = sem("sel_ready")
        stats_done = sem("stats_done")
        mv_done = sem("mv_done")
        var_done = sem("var_done")
        rstd_done = sem("rstd_done")
        z_ready = sem("z_ready")
        t_done = sem("t_done")
        xn_ready = sem("xn_ready")
        qk_done = sem("qk_done")
        v_done = sem("v_done")
        roped = sem("roped")
        qk_summed = sem("qk_summed")
        qk_copied = sem("qk_copied")
        k2_ready = sem("k2_ready")
        qm_ready = sem("qm_ready")
        v_ready = sem("v_ready")
        s_done = sem("s_done")
        max_done = sem("max_done")
        mt_done = sem("mt_done")
        mexp_ready = sem("mexp_ready")
        st_done = sem("st_done")
        p_ready = sem("p_ready")
        av_done = sem("av_done")
        rden_ready = sem("rden_ready")
        rep_done = sem("rep_done")
        rep_copied = sem("rep_copied")
        o_ready = sem("o_ready")
        h_done = sem("h_done")
        gelu_done = sem("gelu_done")
        y_done = sem("y_done")
        gated = sem("gated")
        x_ready = sem("x_ready")
        stored = sem("stored")

        def wt(name):
            a, b = W_COLS[name]
            return w[:, a:b]

        def kind(g):
            return KINDS[g // PAIRS]

        def steps():
            return range(-2, N_ITEMS + LAST_LAG)

        def valid(g):
            return 0 <= g < N_ITEMS

        def attn(g):
            return valid(g) and kind(g) in ATTN

        def ffn(g):
            return valid(g) and kind(g) not in ATTN

        def wait(eng, signal, count):
            if count > 0:
                eng.wait_ge(signal, count)

        MODS = {SELF0: 0, CROSS0: 1, FFN0: 2, SELF1: 3, FFN1: 4}

        def gated_before(g):
            block, pair = divmod(g, PAIRS)
            return sum(k in (SELF1, FFN1) for k in KINDS[:block]) * PAIRS + (pair if KINDS[block] in (SELF1, FFN1) else 0)

        def norms_before(g):
            return g + min(max(g - CROSS1 * PAIRS, 0), PAIRS)

        def attn_upto(g):
            return sum(i <= g for i in ATTN_ITEMS)

        block = stack.enter_context(nc.Block())

        @block.sync
        def _(sp):
            sp.dma_start(x[:], x_d.rearrange("(p t) d -> t p d", p=PAIRS)).then_inc(loaded["x"], 16)
            sp.dma_start(const[:], const_d).then_inc(loaded["const"], 16)
            sp.dma_start(w[:, W_PARTS[0][0]:W_PARTS[0][1]], w_d[:, W_PARTS[0][0]:W_PARTS[0][1]]).then_inc(w_loaded[0], 16)
            sp.dma_start(ln_w[:], lnw_d).then_inc(loaded["mod"], 16)
            sp.dma_start(wmod[:], wmod_d).then_inc(loaded["mod"], 16)
            for n in range(1, len(W_PARTS)):
                a, b = W_PARTS[n]
                sp.dma_start(w[:, a:b], w_d[:, a:b]).then_inc(w_loaded[n], 16)
            out_v = out_d.rearrange("(p t) d -> p t d", p=PAIRS)
            for p in range(PAIRS):
                sp.wait_ge(x_ready, (len(KINDS) - 1) * PAIRS + p + 1)
                sp.dma_start(out_v[p], x[:, p, :]).then_inc(stored, 16)
            sp.wait_ge(stored, 16 * PAIRS)

        @block.gpsimd
        def _(pool):
            nc.gpsimd.memset(K2[:], 0.0).then_inc(zeroed, 1)
            nc.gpsimd.memset(VM[:], 0.0).then_inc(zeroed, 1)
            nc.gpsimd.memset(minus_half[:], -0.5).then_inc(zeroed, 1)
            pool.wait_ge(zeroed, 3)
            pool.wait_ge(loaded["const"], 16)
            den = const[:, C_DEN:C_DEN + 64].rearrange("p (h c) -> p h c", c=8)
            for n in range(4):
                for b in range(2):
                    nc.gpsimd.tensor_copy(VM[:, n, b, :, 64:72], den).then_inc(den_set, 1)

            hp_mask = const[:, C_HP:C_HP + 8].unsqueeze(2).broadcast_to([128, 8, S])

            half_mask = const[:, C_HALF:C_HALF + 2].unsqueeze(2).broadcast_to([128, 2, S])

            def rope_sum(g):
                r, a = rope_index(g), attention_index(g)
                wait(pool, roped, r + 1)
                wait(pool, qm_ready, 2 * (a - 1))
                wait(pool, k2_ready, 2 * (r - 1))
                nc.gpsimd.tensor_tensor(qkT[:, a % 2], t1[:, r % 2], t2[:, r % 2], ALU.add).then_inc(qk_summed, 1)
                wait(pool, st_done, a - 2)
                wait(pool, qk_summed, r + 1)
                for b in range(2):
                    k = qkT[:, a % 2, 1, b, :].unsqueeze(1).broadcast_to([128, 2, S])
                    nc.gpsimd.tensor_tensor(K2[:, a % 3, b], k, half_mask, ALU.mult).then_inc(k2_ready, 1)

            def spread_q(g):
                a = attention_index(g)
                if kind(g) in ROPE:
                    wait(pool, qk_summed, rope_index(g) + 1)
                else:
                    wait(pool, qk_copied, plain_index(g) + 1)
                wait(pool, st_done, a - 2)
                for b in range(2):
                    q = qkT[:, a % 2, 0, b, :].unsqueeze(1).broadcast_to([128, 8, S])
                    nc.gpsimd.tensor_tensor(QM[:, a % 3, b], q, hp_mask, ALU.mult).then_inc(qm_ready, 1)

            def invert_deviation(g):
                before = norms_before(g)
                if g >= 2:
                    wait(pool, z_ready, norms_before(g - 1))
                for i in range(1 + (kind(g) == CROSS1)):
                    wait(pool, var_done, before + i + 1)
                    nc.gpsimd.tensor_tensor(rstd[:, g % 2, i:i + 1], var[:, g % 2, i:i + 1], minus_half[:],
                                            ALU.pow).then_inc(rstd_done, 1)

            for t in steps():
                if valid(t + 1):
                    invert_deviation(t + 1)
                if attn(t - 1):
                    if kind(t - 1) in ROPE:
                        rope_sum(t - 1)
                    spread_q(t - 1)

        @block.scalar
        def _(act):
            act.dma_start(condT[:], condT_d).then_inc(loaded["vec"], 16)
            act.dma_start(vec[:], vec_d).then_inc(loaded["vec"], 16)
            act.dma_start(row[:], row_d).then_inc(loaded["row"], 16)
            act.dma_start(ctxT[:], ctxT_d).then_inc(loaded["ctxT"], 16)
            act.dma_start(ctx[:], ctx_d.rearrange("(p t) d -> t p d", p=PAIRS)).then_inc(loaded["ctx"], 16)
            act.wait_ge(loaded["vec"], 32)
            nc.scalar.activation(siluT[:], condT[:], ACT.Silu).then_inc(silu_done, 1)

            def modulate(g):
                p = g % PAIRS
                wait(act, t_done, g + 1)
                if attn(g - 3):
                    wait(act, v_done, attention_index(g - 3) + 1)
                if ffn(g - 3):
                    wait(act, h_done, ffn_index(g - 3) + 1)
                if kind(g) == CROSS1:
                    nc.scalar.activation(xnT[:, g % 3].rearrange("p c b s -> p (c b s)"), T_ps[:, 0:256],
                                         ACT.Identity).then_inc(xn_ready, 1)
                    return
                if g == 0:
                    act.wait_ge(mod_ready, 10)
                k = MODS[kind(g)]
                for b in range(2):
                    i = nc.scalar.activation(xnT[:, g % 3, 0, b], T_ps[:, S * b:S * b + S], ACT.Identity,
                                             scale=mod_scale[:, k, 2 * p + b:2 * p + b + 1],
                                             bias=mod_shift[:, k, 2 * p + b:2 * p + b + 1])
                i.then_inc(xn_ready, 1)

            def place_qk(g):
                a, n = attention_index(g), plain_index(g)
                bq, bk = {SELF1: (V_Q3, V_K3), CROSS1: (V_Q4, V_K4)}[kind(g)]
                wait(act, qk_done, a + 1)
                wait(act, qm_ready, 2 * (a - 1))
                nc.scalar.activation(qkT[:, a % 2, 0].rearrange("p b s -> p (b s)"), QK_ps[:, 0:128], ACT.Identity,
                                     bias=vec[:, bq:bq + 1])
                wait(act, st_done, a - 2)
                for h2 in range(2):
                    half = slice(64 * h2, 64 * h2 + 64)
                    i = nc.scalar.activation(K2[half, a % 3, :, h2, :],
                                             QK_ps[half, 128:256].rearrange("p (b s) -> p b s", b=2), ACT.Identity,
                                             bias=vec[half, bk:bk + 1])
                i.then_inc(qk_copied, 1)

            def place_v(g):
                a = attention_index(g)
                if a == 0:
                    act.wait_ge(den_set, 8)
                wait(act, v_done, a + 1)
                wait(act, av_done, a - 3)
                for h2 in range(2):
                    half = slice(64 * h2, 64 * h2 + 64)
                    src = VY_ps[half, 0:128].rearrange("p (bg h d) -> p bg h d", bg=4, h=4)
                    dst = tiles_of_v(a % 4, half, h2)
                    i = nc.scalar.activation(dst, src, ACT.Identity)
                i.then_inc(v_ready, 1)

            def tiles_of_v(n, half, h2):
                flat = VM[half, n].rearrange("p b h c -> p (b h c)")
                base = flat[:, 32 * h2:32 * h2 + 1]
                return bass.AP(base.tensor, base.offset, [list(base.ap[0]), [288, 4], [80, 4], [1, 8]])

            def exponentials(g):
                a = attention_index(g)
                wait(act, st_done, a + 1)
                wait(act, av_done, a - 1)
                nc.scalar.activation(P[:, a % 2].rearrange("p b h s -> p (b h s)"), ST_ps[:], ACT.Exp,
                                     scale=SCALE).then_inc(p_ready, 1)

            def gelu(g):
                n = ffn_index(g)
                func, at = ((ACT.Gelu, V_FB1) if kind(g) == FFN0 else (ACT.Gelu_apprx_tanh, V_MB1))
                wait(act, h_done, n + 1)
                if n >= 3:
                    wait(act, y_done, FFN_ITEMS[n - 3] + 1)
                for c in range(FFC):
                    i = nc.scalar.activation(hT[:, n % 3, c], S_ps[:, 128 * c:128 * c + 128], func,
                                             bias=vec[:, at + c:at + c + 1])
                i.then_inc(gelu_done, 1)

            for t in steps():
                if valid(t):
                    modulate(t)
                if attn(t - 1):
                    if kind(t - 1) not in ROPE:
                        place_qk(t - 1)
                    place_v(t - 1)
                if attn(t - 3):
                    exponentials(t - 3)
                if ffn(t - 3):
                    gelu(t - 3)

        @block.vector
        def _(dve):
            dve.wait_ge(loaded["const"], 16)
            nc.vector.tensor_copy(sel[:].rearrange("p b s -> p (b s)"), const[0:16, C_SEL:C_SEL + 256]).then_inc(sel_ready, 1)

            def set_modulation():
                dve.wait_ge(mod_ps_done, 1)
                dve.wait_ge(loaded["vec"], 32)
                for k in range(3):
                    nc.vector.tensor_scalar(mod_scale[:, k], QK_ps[:, 32 * k:32 * k + 16], vec[:, 2 * k:2 * k + 1],
                                            1.0, ALU.add, ALU.add).then_inc(mod_ready, 1)
                    nc.vector.tensor_scalar(mod_shift[:, k], QK_ps[:, 32 * k + 16:32 * k + 32], vec[:, 2 * k + 1:2 * k + 2],
                                            None, ALU.add).then_inc(mod_ready, 1)
                for k, part in ((3, 0), (4, 3)):
                    at = 96 + 32 * (k - 3)
                    nc.vector.tensor_scalar(mod_shift[:, k], QK_ps[:, at:at + 16], vec[:, V_MOD + part:V_MOD + part + 1],
                                            None, ALU.add).then_inc(mod_ready, 1)
                    nc.vector.tensor_scalar(mod_scale[:, k], QK_ps[:, at + 16:at + 32],
                                            vec[:, V_MOD + part + 1:V_MOD + part + 2],
                                            1.0, ALU.add, ALU.add).then_inc(mod_ready, 1)

            def set_rows():
                dve.wait_ge(rows_ps_done, 1)
                nc.vector.tensor_copy(gate[:], O_ps[0:16, 0:256]).then_inc(rows_ready, 1)
                nc.vector.tensor_copy(brow[:].rearrange("p a d -> p (a d)"), O_ps[0:1, 256:512]).then_inc(rows_ready, 1)

            def spread_gates(n):
                dve.wait_ge(gate_ps_done, n + 1)
                nc.vector.tensor_copy(gate_rep[:, 2 * n:2 * n + 2].rearrange("p n a d -> p (n a d)"),
                                      O_ps[:]).then_inc(gate_ready, 1)

            def sources(g):
                return [x] + [ctx] * (kind(g) == CROSS1)

            def statistics(g):
                p, before = g % PAIRS, norms_before(g)
                if g == 0:
                    dve.wait_ge(loaded["x"], 16)
                if g == CROSS1 * PAIRS:
                    dve.wait_ge(loaded["ctx"], 16)
                wait(dve, x_ready, g - PAIRS + 1)
                if g >= 2:
                    wait(dve, z_ready, norms_before(g - 1))
                for i, src in enumerate(sources(g)):
                    nc.vector.bn_stats(stats[:, g % 2, i], src[:, p]).then_inc(stats_done, 1)
                for i, src in enumerate(sources(g)):
                    dve.wait_ge(stats_done, before + i + 1)
                    nc.vector.bn_aggr(mv[:, g % 2, i], stats[:, g % 2, i]).then_inc(mv_done, 1)
                for i, src in enumerate(sources(g)):
                    dve.wait_ge(mv_done, before + i + 1)
                    nc.vector.tensor_scalar(var[:, g % 2, i:i + 1], mv[:, g % 2, i, 1:2], EPS[LAYER[kind(g)]], None,
                                            ALU.add).then_inc(var_done, 1)

            def normalise(g):
                p, before = g % PAIRS, norms_before(g)
                wait(dve, t_done, g - 1)
                for i, src in enumerate(sources(g)):
                    dve.wait_ge(rstd_done, before + i + 1)
                    nc.vector.tensor_scalar(z[:, g % 2, i], src[:, p], mv[:, g % 2, i, 0:1], rstd[:, g % 2, i:i + 1],
                                            ALU.subtract, ALU.mult).then_inc(z_ready, 1)

            def rope(g):
                r, a = rope_index(g), attention_index(g)
                wait(dve, qk_done, a + 1)
                wait(dve, qk_summed, r - 1)
                for at, table, dst in ((0, C_COS, t1), (256, C_SIN, t2)):
                    i = nc.vector.tensor_tensor(dst[:, r % 2].rearrange("p a b s -> p (a b) s"),
                                                QK_ps[:, at:at + 256].rearrange("p (a s) -> p a s", s=S),
                                                const[:, table:table + S].unsqueeze(1).broadcast_to([128, 4, S]), ALU.mult)
                i.then_inc(roped, 1)

            def row_maxima(g):
                a = attention_index(g)
                wait(dve, s_done, a + 1)
                wait(dve, mt_done, a - 1)
                nc.vector.tensor_reduce(m[:, a % 2], S_ps[:].rearrange("p (h k) -> p h k", k=S), AX.X,
                                        ALU.max).then_inc(max_done, 1)

            def spread_maxima(g):
                a = attention_index(g)
                wait(dve, mt_done, a + 1)
                wait(dve, st_done, a - 1)
                nc.vector.tensor_tensor(mexp[:, a % 2], T_ps[0:16, 256:384].unsqueeze(1).broadcast_to([16, 4, 128]),
                                        const[0:16, C_NEG:C_NEG + 4].unsqueeze(2).broadcast_to([16, 4, 128]),
                                        ALU.mult).then_inc(mexp_ready, 1)

            def invert_sums(g):
                a = attention_index(g)
                wait(dve, av_done, a + 1)
                wait(dve, rep_done, a - 1)
                nc.vector.reciprocal(rden[:, a % 2], O_ps[64:72, 0:256]).then_inc(rden_ready, 1)

            def divide(g):
                a = attention_index(g)
                wait(dve, rep_done, a + 1)
                if a >= 2:
                    wait(dve, y_done, ATTN_ITEMS[a - 2] + 1)
                nc.vector.tensor_copy(rep_sb[:, a % 2], O_ps[0:64, 256:512]).then_inc(rep_copied, 1)
                dve.wait_ge(rep_copied, a + 1)
                for G in range(2):
                    i = nc.vector.tensor_tensor(oT[64 * G:64 * G + 64, a % 2].rearrange("p b s -> p (b s)"),
                                                O_ps[0:64, 128 * G:128 * G + 128],
                                                rep_sb[:, a % 2, 128 * G:128 * G + 128], ALU.mult)
                i.then_inc(o_ready, 1)

            def add_residual(g):
                p = g % PAIRS
                wait(dve, y_done, g + 1)
                y = VY_ps[:, 256:384]
                if kind(g) in (SELF1, FFN1):
                    n = gated_before(g)
                    which = 0 if kind(g) == SELF1 else 1
                    nc.vector.tensor_tensor(gy[:, n % 2], y, gate_rep[:, p, which], ALU.mult).then_inc(gated, 1)
                    dve.wait_ge(gated, n + 1)
                    y = gy[:, n % 2]
                nc.vector.tensor_tensor(x[:, p], x[:, p], y, ALU.add).then_inc(x_ready, 1)

            for t in steps():
                if t == 0:
                    set_modulation()
                    set_rows()
                    dve.wait_ge(rows_ready, 2)
                    for n in range(PAIRS // 2):
                        spread_gates(n)
                if attn(t - 3):
                    row_maxima(t - 3)
                    spread_maxima(t - 3)
                if valid(t - 1) and kind(t - 1) in ROPE:
                    rope(t - 1)
                if attn(t - 4):
                    invert_sums(t - 4)
                    divide(t - 4)
                if valid(t - 5):
                    add_residual(t - 5)
                if valid(t + 1):
                    normalise(t + 1)
                if valid(t + 2):
                    statistics(t + 2)

        @block.tensor
        def _(pe):
            def matmul(out, lhsT, rhs, first=True, last=True):
                return nc.tensor.matmul(out, lhsT, rhs, start=first, stop=last)

            def modulation():
                pe.wait_ge(loaded["mod"], 32)
                pe.wait_ge(loaded["vec"], 32)
                pe.wait_ge(loaded["row"], 16)
                pe.wait_ge(loaded["const"], 16)
                pe.wait_ge(silu_done, 1)
                for k in range(6):
                    matmul(QK_ps[:, 16 * k:16 * k + 16], ln_w[:, 128 * k:128 * k + 128], condT[:])
                for n, part in enumerate((0, 1, 3, 4)):
                    i = matmul(QK_ps[:, 96 + 16 * n:112 + 16 * n], wmod[:, 128 * part:128 * part + 128], siluT[:])
                i.then_inc(mod_ps_done, 1)

            def rows():
                ones = const[0:1, C_ONES:C_ONES + 128]
                for n, (part, r) in enumerate(((2, R_GA), (5, R_GM))):
                    matmul(O_ps[0:16, 128 * n:128 * n + 128], siluT[:], wmod[:, 128 * part:128 * part + 128], last=False)
                    matmul(O_ps[0:16, 128 * n:128 * n + 128], ones[:, 0:16], row[:, r:r + 128], first=False)
                for n, (bv, o, r, part) in enumerate(((V_BV3, "o3", R_BP, 3), (V_BV4, "o4", R_BC, 4))):
                    pe.wait_ge(w_loaded[part], 16)
                    matmul(O_ps[0:1, 256 + 128 * n:384 + 128 * n], vec[:, bv:bv + 1], wt(o), last=False)
                    i = matmul(O_ps[0:1, 256 + 128 * n:384 + 128 * n], ones[:, 0:1], row[:, r:r + 128], first=False)
                i.then_inc(rows_ps_done, 1)

            def gates():
                pe.wait_ge(rows_ready, 2)
                for n in range(PAIRS // 2):
                    wait(pe, gate_ready, n)
                    for j in range(2):
                        p = 2 * n + j
                        i = matmul(O_ps[:, 256 * j:256 * j + 256],
                                   const[0:16, C_PAIR + 128 * p:C_PAIR + 128 * p + 128], gate[:])
                    i.then_inc(gate_ps_done, 1)

            def turn_input(g):
                wait(pe, z_ready, norms_before(g) + 1 + (kind(g) == CROSS1))
                wait(pe, xn_ready, g)
                wait(pe, mexp_ready, attn_upto(g - 4))
                n = 1 + (kind(g) == CROSS1)
                for i in range(n):
                    mm = nc.tensor.transpose(T_ps[:, 128 * i:128 * i + 128], z[:, g % 2, i], ident)
                mm.then_inc(t_done, 1)

            def turn_maxima(g):
                a = attention_index(g)
                wait(pe, max_done, a + 1)
                wait(pe, xn_ready, min(g + 4, N_ITEMS))
                nc.tensor.transpose(T_ps[0:16, 256:384], m[:, a % 2], ident).then_inc(mt_done, 1)

            def project(g):
                k, a, p = kind(g), attention_index(g), g % PAIRS
                pe.wait_ge(xn_ready, g + 1)
                if p == 0:
                    pe.wait_ge(w_loaded[k], 16)
                if g == CROSS0 * PAIRS:
                    pe.wait_ge(loaded["ctxT"], 16)
                if g == 0:
                    pe.wait_ge(mod_ready, 10)
                xin = xnT[:, g % 3, 0].rearrange("p b s -> p (b s)")
                kv = {SELF0: xin, SELF1: xin, CROSS0: ctxT[:, p].rearrange("p b s -> p (b s)"),
                      CROSS1: xnT[:, g % 3, 1].rearrange("p b s -> p (b s)")}[k]
                if k in ROPE:
                    wait(pe, roped, rope_index(g))
                else:
                    wait(pe, roped, 2 * PAIRS)
                    wait(pe, qk_copied, plain_index(g))
                parts = [("q", xin, 0), ("k", kv, 128)] + [("qs", xin, 256), ("ks", kv, 384)] * (k in ROPE)
                for name, rhs, at in parts:
                    i = matmul(QK_ps[:, at:at + 128], wt(f"{name}{k}"), rhs)
                i.then_inc(qk_done, 1)
                wait(pe, v_ready, a)
                wait(pe, x_ready, g - 4)
                for h2 in range(2):
                    for b in range(2):
                        i = matmul(VY_ps[64 * h2:64 * h2 + 64, 64 * b:64 * b + 64], kv[:, 64 * b:64 * b + 64],
                                   wt(f"v{k}")[:, 64 * h2:64 * h2 + 64])
                i.then_inc(v_done, 1)
                return i

            def scores_by_query(g):
                a = attention_index(g)
                wait(pe, qm_ready, 2 * (a + 1))
                if kind(g) in ROPE:
                    wait(pe, k2_ready, 2 * (rope_index(g) + 1))
                else:
                    wait(pe, qk_copied, plain_index(g) + 1)
                wait(pe, max_done, a)
                wait(pe, gelu_done, ffn_index(g))
                for b in range(2):
                    for j in range(4):
                        at = 512 * b + 128 * j
                        i = matmul(S_ps[:, at:at + 128], QM[:, a % 3, b, 2 * j:2 * j + 2].rearrange("p h s -> p (h s)"),
                                   K2[:, a % 3, b].rearrange("p h s -> p (h s)"))
                i.then_inc(s_done, 1)

            def scores_by_key(g):
                a = attention_index(g)
                wait(pe, mexp_ready, a + 1)
                wait(pe, p_ready, a)
                if a == 0:
                    pe.wait_ge(sel_ready, 1)
                for b in range(2):
                    out = ST_ps[:, 512 * b:512 * b + 512]
                    matmul(out, K2[:, a % 3, b].rearrange("p h s -> p (h s)"),
                           QM[:, a % 3, b].rearrange("p h s -> p (h s)"), last=False)
                    i = matmul(out, sel[:, b], mexp[:, a % 2].rearrange("p j s -> p (j s)"), first=False)
                i.then_inc(st_done, 1)

            def weigh_values(g):
                a = attention_index(g)
                wait(pe, p_ready, a + 1)
                wait(pe, v_ready, a + 1)
                wait(pe, o_ready, a)
                if a == 0:
                    pe.wait_ge(gate_ready, PAIRS // 2)
                for G in range(2):
                    for b in range(2):
                        out = O_ps[0:72, 128 * G + 64 * b:128 * G + 64 * b + 64]
                        for hp4 in range(4):
                            hp = 4 * G + hp4
                            i = matmul(out, VM[:, a % 4, b, hp], P[:, a % 2, b, hp], hp4 == 0, hp4 == 3)
                i.then_inc(av_done, 1)

            def spread_sums(g):
                a = attention_index(g)
                wait(pe, rden_ready, a + 1)
                matmul(O_ps[0:64, 256:512], const[0:8, C_REP:C_REP + 64], rden[:, a % 2]).then_inc(rep_done, 1)

            def first_product(g):
                n = ffn_index(g)
                pe.wait_ge(xn_ready, g + 1)
                if g % PAIRS == 0:
                    pe.wait_ge(w_loaded[kind(g)], 16)
                wait(pe, max_done, attention_index(g))
                wait(pe, gelu_done, n)
                for c in range(FFC):
                    i = matmul(S_ps[:, 128 * c:128 * c + 128], wt(f"w1_{kind(g)}")[:, 128 * c:128 * c + 128],
                               xnT[:, g % 3, 0].rearrange("p b s -> p (b s)"))
                i.then_inc(h_done, 1)

            def block_output(g):
                k = kind(g)
                y = VY_ps[:, 256:384]
                wait(pe, v_ready, attn_upto(g + 4))
                wait(pe, x_ready, g)
                if k in ATTN:
                    a = attention_index(g)
                    wait(pe, o_ready, a + 1)
                    i = matmul(y, oT[:, a % 2].rearrange("p b s -> p (b s)"), wt(f"o{k}"), last=k in ROPE)
                    bias = {SELF1: brow[:, 0], CROSS1: brow[:, 1]}.get(k)
                else:
                    n = ffn_index(g)
                    wait(pe, gelu_done, n + 1)
                    for c in range(FFC):
                        matmul(y, hT[:, n % 3, c], wt(f"w2_{k}")[:, 128 * c:128 * c + 128], c == 0, False)
                    r = R_FB2 if k == FFN0 else R_MB2
                    bias = row[:, r:r + 128]
                if bias is not None:
                    i = matmul(y, const[0:1, C_ONES:C_ONES + 128], bias, first=False)
                i.then_inc(y_done, 1)

            modulation()
            rows()
            gates()
            for t in steps():
                if valid(t):
                    turn_input(t)
                if attn(t - 1):
                    project(t - 1)
                if attn(t - 3):
                    turn_maxima(t - 3)
                if attn(t - 4):
                    weigh_values(t - 4)
                if attn(t - 3):
                    scores_by_key(t - 3)
                if attn(t - 2):
                    scores_by_query(t - 2)
                if ffn(t - 2):
                    first_product(t - 2)
                if attn(t - 4):
                    spread_sums(t - 4)
                if valid(t - 5):
                    block_output(t - 5)


def _packed_weights(i):
    def swapped(wt):
        return wt.reshape(D, H, 2, HD // 2)[:, :, ::-1].reshape(D, D)

    def by_tiles(wt):
        return wt.reshape(2, 2, 4, HD, -1).transpose(1, 0, 2, 3, 4).reshape(D, -1)

    def chunks(wt):
        return wt.reshape(FFC, 128, D).transpose(1, 0, 2).reshape(128, FFC * D)

    def L0(name):
        return i["L0_xcond_" + name].T

    def L1(name):
        return i["L1_xcond_" + name]

    blocks = {"v0": L0("qkv_w")[:, 256:], "o0": by_tiles(L0("sa_out_w")), "v1": L0("v_w"), "o1": by_tiles(L0("ca_out_w")),
              "w1_2": L0("ffn_w1"), "w2_2": chunks(L0("ffn_w2")),
              "q3": L1("W_qkv")[:, :128], "k3": L1("W_qkv")[:, 128:256], "v3": L1("W_qkv")[:, 256:],
              "o3": by_tiles(L1("W_proj")), "q4": L1("W_qc"), "k4": L1("W_kvc")[:, :128], "v4": L1("W_kvc")[:, 128:],
              "o4": by_tiles(L1("W_cproj")), "w1_5": L1("W_mlp1"), "w2_5": chunks(L1("W_mlp2"))}
    for n, (q, k) in enumerate(((L0("qkv_w")[:, :128], L0("qkv_w")[:, 128:256]), (L0("q_w"), L0("k_w")))):
        blocks.update({f"q{n}": q, f"k{n}": k, f"qs{n}": swapped(q), f"ks{n}": swapped(k)})
    return np.concatenate([blocks[name] for name in W_COLS], axis=1)


def _packed_vectors(i):
    def by_tiles(v):
        return v.reshape(2, 2, 4, HD).transpose(1, 0, 2, 3).reshape(D)

    cols = []
    for n in (1, 2, 3):
        cols += list(i[f"L0_xcond_ln{n}_b"].reshape(2, D))
    cols += list(i["L1_xcond_b_mod"].reshape(6, D))
    cols += list(i["L0_xcond_ffn_b1"].reshape(FFC, 128))
    cols += list(i["L1_xcond_b_mlp1"].reshape(FFC, 128))
    qkv, kv = i["L1_xcond_b_qkv"].reshape(3, D), i["L1_xcond_b_kvc"].reshape(2, D)
    cols += [qkv[0], qkv[1], i["L1_xcond_b_qc"], kv[0], by_tiles(qkv[2]), by_tiles(kv[1])]
    mod = i["L1_xcond_b_mod"].reshape(6, D)
    rows = [i["L0_xcond_ffn_b2"], i["L1_xcond_b_proj"], i["L1_xcond_b_cproj"], i["L1_xcond_b_mlp2"], mod[2], mod[5]]
    return np.stack(cols, axis=1), np.concatenate(rows)[None, :]


def kernel(**inputs):
    import concourse.bacc as bacc
    from concourse.bass_utils import run_bass_kernel_spmd

    i = {k: np.asarray(v) for k, v in inputs.items()}
    vec, row = _packed_vectors(i)
    ctx = i["ctx_1024"].reshape(B * S, D)
    arrays = {
        "x": i["x"].reshape(B * S, D),
        "ctx": ctx,
        "ctxT": ctx.T.reshape(D, PAIRS, 2, S),
        "condT": i["cond_1024"].T,
        "w": _packed_weights(i),
        "lnw": np.concatenate([i[f"L0_xcond_ln{n}_w"].T for n in (1, 2, 3)], axis=1),
        "wmod": i["L1_xcond_W_mod"],
        "vec": vec,
        "row": row,
        "const": _constants(),
    }
    nc = bacc.Bacc("TRN2", target_bir_lowering=False, num_devices=1)
    ins, args = {}, []
    for name, a in arrays.items():
        ins[f"in_{name}"] = np.ascontiguousarray(a)
        args.append(nc.dram_tensor(f"in_{name}", a.shape, F32, kind="ExternalInput").ap())
    args.append(nc.dram_tensor("out_x", (B * S, D), F32, kind="ExternalOutput").ap())
    build(nc, *args)
    r = run_bass_kernel_spmd(nc, [ins], core_ids=[0])
    return r.results[0]["out_x"].reshape(B, S, D)
```

```python
from contextlib import ExitStack

import numpy as np

import concourse.bass as bass
from concourse import mybir

F32 = mybir.dt.float32
F32R = mybir.dt.float32r
ALU = mybir.AluOpType
ACT = mybir.ActivationFunctionType
AX = mybir.AxisListType

B, S, D = 16, 64, 128
H, HD = 16, 8
FF = 512
PAIRS = B // 2
FFC = FF // 128
SCALE = HD ** -0.5
EPS = {0: 1e-5, 1: 1e-6}

SELF0, CROSS0, FFN0, SELF1, CROSS1, FFN1 = range(6)
KINDS = [SELF0, CROSS0, FFN0, SELF1, CROSS1, FFN1]
LAYER = {SELF0: 0, CROSS0: 0, FFN0: 0, SELF1: 1, CROSS1: 1, FFN1: 1}
ATTN = (SELF0, CROSS0, SELF1, CROSS1)
ROPE = (SELF0, CROSS0)
N_ITEMS = len(KINDS) * PAIRS
GATES_STEP = FFN0 * PAIRS + 6
LAST_LAG = 5

W_COLS = {}


def _w_columns():
    at = 0
    for name, n in (("q0", 128), ("k0", 128), ("qs0", 128), ("ks0", 128), ("v0", 128), ("o0", 128),
                    ("q1", 128), ("k1", 128), ("qs1", 128), ("ks1", 128), ("v1", 128), ("o1", 128),
                    ("w1_2", FF), ("w2_2", FF),
                    ("q3", 128), ("k3", 128), ("v3", 128), ("o3", 128),
                    ("q4", 128), ("k4", 128), ("v4", 128), ("o4", 128),
                    ("w1_5", FF), ("w2_5", FF)):
        W_COLS[name] = (at, at + n)
        at += n
    return at


W_N = _w_columns()
W_PARTS = [(0, W_COLS["o0"][1]), (W_COLS["q1"][0], W_COLS["o1"][1]), (W_COLS["w1_2"][0], W_COLS["w2_2"][1]),
           (W_COLS["q3"][0], W_COLS["o3"][1]), (W_COLS["q4"][0], W_COLS["o4"][1]),
           (W_COLS["w1_5"][0], W_COLS["w2_5"][1])]

V_LN = 0
V_MOD = 6
V_FB1 = 12
V_MB1 = 16
V_Q3, V_K3, V_Q4, V_K4 = 20, 21, 22, 23
V_BV3, V_BV4 = 24, 25
V_N = 26
R_FB2, R_BP, R_BC, R_MB2, R_GA, R_GM, R_N = 0, 128, 256, 384, 512, 640, 768

C_ID, C_COS, C_SIN, C_HP, C_DEN, C_N = 0, 128, 192, 256, 264, 328
F_NEG, F_SEL, F_REP, F_PAIR, F_ONES, F_N = 0, 4, 260, 324, 1348, 1476


def _constants():
    c = np.zeros((128, C_N), np.float32)
    f = np.zeros((16, F_N), np.float32)
    c[:, C_ID:C_ID + 128] = np.eye(128, dtype=np.float32)
    half = HD // 2
    inv_freq = (np.float32(1.0) / np.power(np.float32(10000.0), np.arange(half, dtype=np.float32) / half)).astype(np.float32)
    ang = np.arange(S, dtype=np.float32)[:, None] * inv_freq[None, :]
    p = np.arange(128)
    c[:, C_COS:C_COS + S] = np.cos(ang).astype(np.float32).T[p % half]
    sign = np.where(p % HD < half, np.float32(-1), np.float32(1))[:, None]
    c[:, C_SIN:C_SIN + S] = sign * np.sin(ang).astype(np.float32).T[p % half]
    c[p, C_HP + (p // HD) % 8] = 1.0
    for b in range(2):
        for j in range(4):
            for h2 in range(2):
                r = b * 8 + j * 2 + h2
                f[r, F_NEG + j] = -1.0
                f[r, F_SEL + b * 128 + h2 * 64:F_SEL + b * 128 + h2 * 64 + 64] = 1.0
    for r in range(8):
        f[r, F_REP + 8 * r:F_REP + 8 * r + 8] = 1.0
    for b in range(B):
        f[b, F_PAIR + b * S:F_PAIR + (b + 1) * S] = 1.0
    f[:, F_ONES:] = 1.0
    for hp in range(8):
        c[:64, C_DEN + hp * 8 + hp % 4] = 1.0
        c[64:, C_DEN + hp * 8 + 4 + hp % 4] = 1.0
    return c, f


def attention_index(g):
    block, pair = divmod(g, PAIRS)
    return sum(k in ATTN for k in KINDS[:block]) * PAIRS + (pair if KINDS[block] in ATTN else 0)


def ffn_index(g):
    block, pair = divmod(g, PAIRS)
    return sum(k not in ATTN for k in KINDS[:block]) * PAIRS + (pair if KINDS[block] not in ATTN else 0)


def plain_index(g):
    block, pair = divmod(g, PAIRS)
    return sum(k in (SELF1, CROSS1) for k in KINDS[:block]) * PAIRS + (pair if KINDS[block] in (SELF1, CROSS1) else 0)


def rope_index(g):
    block, pair = divmod(g, PAIRS)
    return sum(k in ROPE for k in KINDS[:block]) * PAIRS + (pair if KINDS[block] in ROPE else 0)


ATTN_ITEMS = [g for g in range(N_ITEMS) if KINDS[g // PAIRS] in ATTN]
FFN_ITEMS = [g for g in range(N_ITEMS) if KINDS[g // PAIRS] not in ATTN]


def build(nc, x_d, ctx_d, ctxT_d, condT_d, w_d, lnw_d, wmod_d, vec_d, row_d, const_d, few_d, out_d):
    with ExitStack() as stack:
        def sb(name, shape, dt=F32):
            return stack.enter_context(nc.sbuf_tensor(name, shape, dt))

        def ps(name, shape):
            return stack.enter_context(nc.psum_tensor(name, shape, F32))

        def sem(name):
            return stack.enter_context(nc.semaphore(name))

        x = sb("x", [128, PAIRS, D])
        ctx = sb("ctx", [128, PAIRS, D])
        ctxT = sb("ctxT", [D, PAIRS, 2, S])
        w = sb("w", [128, W_N])
        wmod = sb("wmod", [D, 6 * D])
        ln_w = sb("ln_w", [D, 6 * D])
        vec = sb("vec", [D, V_N])
        row = sb("row", [1, R_N])
        const = sb("const", [128, C_N])
        few = sb("few", [16, F_N])
        condT = sb("condT", [D, B])
        sel = sb("sel", [16, 2, 128], F32R)
        mod_scale = sb("mod_scale", [D, 5, B])
        mod_shift = sb("mod_shift", [D, 5, B])
        siluT = sb("siluT", [D, B])
        gate = sb("gate", [B, 2 * D])
        gate_rep = sb("gate_rep", [128, PAIRS, 2, D])
        brow = sb("brow", [1, 2, D])
        stats = sb("stats", [128, 2, 2, 6])
        mv = sb("mv", [128, 2, 2, 2])
        var = sb("var", [128, 2, 2])
        rstd = sb("rstd", [128, 2, 2])
        minus_half = sb("minus_half", [128, 1])
        z = sb("z", [128, 2, 2, D])
        xnT = sb("xnT", [D, 3, 2, 2, S])
        t1 = sb("t1", [128, 2, 2, 2, S])
        t2 = sb("t2", [128, 2, 2, 2, S])
        qkT = sb("qkT", [128, 2, 2, 2, S])
        parts = sb("parts", [128, 2, 2, 2, 2, S], F32R)
        QM = sb("QM", [128, 3, 2, 2, 8, S], F32R)
        K2 = sb("K2", [128, 3, 2, 2, 2, S], F32R)
        VM = sb("VM", [128, 4, 2, 8, 72])
        m = sb("m", [128, 2, 16])
        mexp = sb("mexp", [16, 2, 4, 128], F32R)
        P = sb("P", [128, 2, 2, 8, S])
        rden = sb("rden", [8, 2, 256])
        rden_rows = sb("rden_rows", [64, 2, 256])
        oT = sb("oT", [128, 2, 2, S])
        hT = sb("hT", [128, 3, FFC, 128])
        gy = sb("gy", [128, 2, D])
        T_ps = ps("T_ps", [128, 512])
        QK_ps = ps("QK_ps", [128, 512])
        VY_ps = ps("VY_ps", [128, 512])
        O_ps = ps("O_ps", [128, 512])
        S_ps = ps("S_ps", [128, 1024])
        ST_ps = ps("ST_ps", [128, 1024])

        ident = const[:, C_ID:C_ID + 128]

        loaded = {n: sem(f"loaded_{n}") for n in ("x", "ctx", "ctxT", "const", "few", "vec", "lnw", "mod", "row")}
        w_loaded = [sem(f"w_loaded_{n}") for n in range(len(W_PARTS))]
        zeroed = sem("zeroed")
        den_set = sem("den_set")
        silu_done = sem("silu_done")
        mod_ps_done = sem("mod_ps_done")
        mod_ready = sem("mod_ready")
        rows_ps_done = sem("rows_ps_done")
        rows_ready = sem("rows_ready")
        gate_ps_done = sem("gate_ps_done")
        gate_ready = sem("gate_ready")
        sel_ready = sem("sel_ready")
        stats_done = sem("stats_done")
        mv_done = sem("mv_done")
        var_done = sem("var_done")
        rstd_done = sem("rstd_done")
        z_ready = sem("z_ready")
        t_done = sem("t_done")
        xn_ready = sem("xn_ready")
        qk_done = sem("qk_done")
        v_done = sem("v_done")
        roped = sem("roped")
        qk_summed = sem("qk_summed")
        qk_copied = sem("qk_copied")
        high_ready = sem("high_ready")
        rest_ready = sem("rest_ready")
        k2_ready = sem("k2_ready")
        qm_ready = sem("qm_ready")
        v_ready = sem("v_ready")
        s_done = sem("s_done")
        max_done = sem("max_done")
        mt_done = sem("mt_done")
        mexp_ready = sem("mexp_ready")
        st_done = sem("st_done")
        p_ready = sem("p_ready")
        av_done = sem("av_done")
        rden_ready = sem("rden_ready")
        rep_done = sem("rep_done")
        rep_copied = sem("rep_copied")
        o_ready = sem("o_ready")
        h_done = sem("h_done")
        gelu_done = sem("gelu_done")
        y_done = sem("y_done")
        gated = sem("gated")
        x_ready = sem("x_ready")
        stored = sem("stored")

        def wt(name):
            a, b = W_COLS[name]
            return w[:, a:b]

        def kind(g):
            return KINDS[g // PAIRS]

        def steps():
            return range(-2, N_ITEMS + LAST_LAG)

        def valid(g):
            return 0 <= g < N_ITEMS

        def attn(g):
            return valid(g) and kind(g) in ATTN

        def ffn(g):
            return valid(g) and kind(g) not in ATTN

        def wait(eng, signal, count):
            if count > 0:
                eng.wait_ge(signal, count)

        MODS = {SELF0: 0, CROSS0: 1, FFN0: 2, SELF1: 3, FFN1: 4}

        def gated_before(g):
            block, pair = divmod(g, PAIRS)
            return sum(k in (SELF1, FFN1) for k in KINDS[:block]) * PAIRS + (pair if KINDS[block] in (SELF1, FFN1) else 0)

        def norms_before(g):
            return g + min(max(g - CROSS1 * PAIRS, 0), PAIRS)

        def attn_upto(g):
            return sum(i <= g for i in ATTN_ITEMS)

        block = stack.enter_context(nc.Block())

        @block.sync
        def _(sp):
            sp.dma_start(x[:], x_d.rearrange("(p t) d -> t p d", p=PAIRS)).then_inc(loaded["x"], 16)
            sp.dma_start(ln_w[:], lnw_d).then_inc(loaded["lnw"], 16)
            for n in range(len(W_PARTS)):
                a, b = W_PARTS[n]
                sp.dma_start(w[:, a:b], w_d[:, a:b]).then_inc(w_loaded[n], 16)
                if n == 1:
                    sp.dma_start(ctxT[:], ctxT_d).then_inc(loaded["ctxT"], 16)
            sp.dma_start(wmod[:], wmod_d).then_inc(loaded["mod"], 16)
            sp.dma_start(ctx[:], ctx_d.rearrange("(p t) d -> t p d", p=PAIRS)).then_inc(loaded["ctx"], 16)
            out_v = out_d.rearrange("(p t) d -> p t d", p=PAIRS)
            for p in range(PAIRS):
                sp.wait_ge(x_ready, (len(KINDS) - 1) * PAIRS + p + 1)
                sp.dma_start(out_v[p], x[:, p, :]).then_inc(stored, 16)
            sp.wait_ge(stored, 16 * PAIRS)

        @block.gpsimd
        def _(pool):
            nc.gpsimd.memset(K2[:].bitcast(F32), 0.0).then_inc(zeroed, 1)
            nc.gpsimd.memset(VM[:], 0.0).then_inc(zeroed, 1)
            nc.gpsimd.memset(minus_half[:], -0.5).then_inc(zeroed, 1)
            pool.wait_ge(zeroed, 3)
            pool.wait_ge(loaded["const"], 16)
            den = const[:, C_DEN:C_DEN + 64].rearrange("p (h c) -> p h c", c=8)
            for n in range(4):
                for b in range(2):
                    nc.gpsimd.tensor_copy(VM[:, n, b, :, 64:72], den).then_inc(den_set, 1)

            hp_mask = const[:, C_HP:C_HP + 8].unsqueeze(2).broadcast_to([128, 8, S])

            def rope_sum(g):
                r, a = rope_index(g), attention_index(g)
                wait(pool, roped, r + 1)
                wait(pool, rest_ready, a - 1)
                nc.gpsimd.tensor_tensor(qkT[:, a % 2], t1[:, r % 2], t2[:, r % 2], ALU.add).then_inc(qk_summed, 1)

            def spread_q(g):
                a = attention_index(g)
                wait(pool, st_done, a - 2)
                for part, ready in ((0, high_ready), (1, rest_ready)):
                    wait(pool, ready, a + 1)
                    for b in range(2):
                        q = parts[:, a % 2, part, 0, b, :].bitcast(F32).unsqueeze(1).broadcast_to([128, 8, S])
                        nc.gpsimd.tensor_tensor(QM[:, a % 3, part, b], q, hp_mask, ALU.mult).then_inc(qm_ready, 1)

            def invert_deviation(g):
                before = norms_before(g)
                if g >= 2:
                    wait(pool, z_ready, norms_before(g - 1))
                for i in range(1 + (kind(g) == CROSS1)):
                    wait(pool, var_done, before + i + 1)
                    nc.gpsimd.tensor_tensor(rstd[:, g % 2, i:i + 1], var[:, g % 2, i:i + 1], minus_half[:],
                                            ALU.pow).then_inc(rstd_done, 1)

            for t in steps():
                if valid(t + 1):
                    invert_deviation(t + 1)
                if attn(t - 1):
                    if kind(t - 1) in ROPE:
                        rope_sum(t - 1)
                    spread_q(t - 1)

        @block.scalar
        def _(act):
            act.dma_start(condT[:], condT_d).then_inc(loaded["vec"], 16)
            act.dma_start(vec[:], vec_d).then_inc(loaded["vec"], 16)
            act.dma_start(const[:], const_d).then_inc(loaded["const"], 16)
            act.dma_start(few[:], few_d).then_inc(loaded["few"], 16)
            act.dma_start(row[:], row_d).then_inc(loaded["row"], 16)
            act.wait_ge(loaded["vec"], 32)
            nc.scalar.activation(siluT[:], condT[:], ACT.Silu).then_inc(silu_done, 1)

            def modulate(g):
                p = g % PAIRS
                wait(act, t_done, g + 1)
                if attn(g - 3):
                    wait(act, v_done, attention_index(g - 3) + 1)
                if ffn(g - 3):
                    wait(act, h_done, ffn_index(g - 3) + 1)
                if kind(g) == CROSS1:
                    nc.scalar.activation(xnT[:, g % 3].rearrange("p c b s -> p (c b s)"), T_ps[:, 0:256],
                                         ACT.Identity).then_inc(xn_ready, 1)
                    return
                if g == 0:
                    act.wait_ge(mod_ready, 6)
                if g == SELF1 * PAIRS:
                    act.wait_ge(mod_ready, 10)
                k = MODS[kind(g)]
                for b in range(2):
                    i = nc.scalar.activation(xnT[:, g % 3, 0, b], T_ps[:, S * b:S * b + S], ACT.Identity,
                                             scale=mod_scale[:, k, 2 * p + b:2 * p + b + 1],
                                             bias=mod_shift[:, k, 2 * p + b:2 * p + b + 1])
                i.then_inc(xn_ready, 1)

            def add_qk_bias(g):
                a = attention_index(g)
                wait(act, qk_done, a + 1)
                wait(act, rest_ready, a - 1)
                for n, bias in enumerate({SELF1: (V_Q3, V_K3), CROSS1: (V_Q4, V_K4)}[kind(g)]):
                    i = nc.scalar.activation(qkT[:, a % 2, n].rearrange("p b s -> p (b s)"),
                                             QK_ps[:, 128 * n:128 * n + 128], ACT.Identity, bias=vec[:, bias:bias + 1])
                i.then_inc(qk_copied, 1)

            def high_parts(g):
                a = attention_index(g)
                if kind(g) in ROPE:
                    wait(act, qk_summed, rope_index(g) + 1)
                else:
                    wait(act, qk_copied, plain_index(g) + 1)
                wait(act, qm_ready, 4 * (a - 1))
                wait(act, k2_ready, a - 1)
                nc.scalar.activation(parts[:, a % 2, 0].rearrange("p n b s -> p (n b s)"),
                                     qkT[:, a % 2].rearrange("p n b s -> p (n b s)"), ACT.Identity).then_inc(high_ready, 1)

            def place_k(g):
                a = attention_index(g)
                if a == 0:
                    act.wait_ge(zeroed, 3)
                wait(act, rest_ready, a + 1)
                wait(act, st_done, a - 2)
                for h2 in range(2):
                    half = slice(64 * h2, 64 * h2 + 64)
                    i = nc.scalar.activation(K2[half, a % 3, :, :, h2, :], parts[half, a % 2, :, 1].bitcast(F32),
                                             ACT.Identity)
                i.then_inc(k2_ready, 1)

            def place_v(g):
                a = attention_index(g)
                if a == 0:
                    act.wait_ge(den_set, 8)
                wait(act, v_done, a + 1)
                wait(act, av_done, a - 3)
                for h2 in range(2):
                    half = slice(64 * h2, 64 * h2 + 64)
                    src = VY_ps[half, 0:128].rearrange("p (bg h d) -> p bg h d", bg=4, h=4)
                    dst = tiles_of_v(a % 4, half, h2)
                    i = nc.scalar.activation(dst, src, ACT.Identity)
                i.then_inc(v_ready, 1)

            def tiles_of_v(n, half, h2):
                flat = VM[half, n].rearrange("p b h c -> p (b h c)")
                base = flat[:, 32 * h2:32 * h2 + 1]
                return bass.AP(base.tensor, base.offset, [list(base.ap[0]), [288, 4], [80, 4], [1, 8]])

            def exponentials(g):
                a = attention_index(g)
                wait(act, st_done, a + 1)
                wait(act, av_done, a - 1)
                nc.scalar.activation(P[:, a % 2].rearrange("p b h s -> p (b h s)"), ST_ps[:], ACT.Exp,
                                     scale=SCALE).then_inc(p_ready, 1)

            def copy_inverses(g):
                a = attention_index(g)
                wait(act, rep_done, a + 1)
                wait(act, o_ready, a - 1)
                nc.scalar.activation(rden_rows[:, a % 2], O_ps[0:64, 256:512], ACT.Identity).then_inc(rep_copied, 1)

            def gelu(g):
                n = ffn_index(g)
                func, at = ((ACT.Gelu, V_FB1) if kind(g) == FFN0 else (ACT.Gelu_apprx_tanh, V_MB1))
                wait(act, h_done, n + 1)
                if n >= 3:
                    wait(act, y_done, FFN_ITEMS[n - 3] + 1)
                for c in range(FFC):
                    i = nc.scalar.activation(hT[:, n % 3, c], S_ps[:, 128 * c:128 * c + 128], func,
                                             bias=vec[:, at + c:at + c + 1])
                i.then_inc(gelu_done, 1)

            for t in steps():
                if valid(t):
                    modulate(t)
                if attn(t - 1):
                    if kind(t - 1) not in ROPE:
                        add_qk_bias(t - 1)
                    place_v(t - 1)
                    high_parts(t - 1)
                    place_k(t - 1)
                if attn(t - 3):
                    exponentials(t - 3)
                if ffn(t - 3):
                    gelu(t - 3)
                if attn(t - 4):
                    copy_inverses(t - 4)

        @block.vector
        def _(dve):
            dve.wait_ge(loaded["const"], 16)
            dve.wait_ge(loaded["few"], 16)
            nc.vector.tensor_copy(sel[:].rearrange("p b s -> p (b s)"), few[:, F_SEL:F_SEL + 256]).then_inc(sel_ready, 1)

            def set_modulation():
                dve.wait_ge(mod_ps_done, 1)
                dve.wait_ge(loaded["vec"], 32)
                for k in range(3):
                    nc.vector.tensor_scalar(mod_scale[:, k], QK_ps[:, 32 * k:32 * k + 16], vec[:, 2 * k:2 * k + 1],
                                            1.0, ALU.add, ALU.add).then_inc(mod_ready, 1)
                    nc.vector.tensor_scalar(mod_shift[:, k], QK_ps[:, 32 * k + 16:32 * k + 32], vec[:, 2 * k + 1:2 * k + 2],
                                            None, ALU.add).then_inc(mod_ready, 1)

            def set_modulation_dit():
                dve.wait_ge(mod_ps_done, 2)
                for k, part in ((3, 0), (4, 3)):
                    at = 96 + 32 * (k - 3)
                    nc.vector.tensor_scalar(mod_shift[:, k], QK_ps[:, at:at + 16], vec[:, V_MOD + part:V_MOD + part + 1],
                                            None, ALU.add).then_inc(mod_ready, 1)
                    nc.vector.tensor_scalar(mod_scale[:, k], QK_ps[:, at + 16:at + 32],
                                            vec[:, V_MOD + part + 1:V_MOD + part + 2],
                                            1.0, ALU.add, ALU.add).then_inc(mod_ready, 1)

            def set_rows():
                dve.wait_ge(rows_ps_done, 1)
                nc.vector.tensor_copy(gate[:], O_ps[0:16, 0:256]).then_inc(rows_ready, 1)
                nc.vector.tensor_copy(brow[:].rearrange("p a d -> p (a d)"), O_ps[0:1, 256:512]).then_inc(rows_ready, 1)

            def spread_gates(n):
                dve.wait_ge(gate_ps_done, n + 1)
                nc.vector.tensor_copy(gate_rep[:, 2 * n:2 * n + 2].rearrange("p n a d -> p (n a d)"),
                                      O_ps[:]).then_inc(gate_ready, 1)

            def sources(g):
                return [x] + [ctx] * (kind(g) == CROSS1)

            def statistics(g):
                p, before = g % PAIRS, norms_before(g)
                if g == 0:
                    dve.wait_ge(loaded["x"], 16)
                if g == CROSS1 * PAIRS:
                    dve.wait_ge(loaded["ctx"], 16)
                wait(dve, x_ready, g - PAIRS + 1)
                if g >= 2:
                    wait(dve, z_ready, norms_before(g - 1))
                for i, src in enumerate(sources(g)):
                    nc.vector.bn_stats(stats[:, g % 2, i], src[:, p]).then_inc(stats_done, 1)
                for i, src in enumerate(sources(g)):
                    dve.wait_ge(stats_done, before + i + 1)
                    nc.vector.bn_aggr(mv[:, g % 2, i], stats[:, g % 2, i]).then_inc(mv_done, 1)
                for i, src in enumerate(sources(g)):
                    dve.wait_ge(mv_done, before + i + 1)
                    nc.vector.tensor_scalar(var[:, g % 2, i:i + 1], mv[:, g % 2, i, 1:2], EPS[LAYER[kind(g)]], None,
                                            ALU.add).then_inc(var_done, 1)

            def normalise(g):
                p, before = g % PAIRS, norms_before(g)
                wait(dve, t_done, g - 1)
                for i, src in enumerate(sources(g)):
                    dve.wait_ge(rstd_done, before + i + 1)
                    nc.vector.tensor_scalar(z[:, g % 2, i], src[:, p], mv[:, g % 2, i, 0:1], rstd[:, g % 2, i:i + 1],
                                            ALU.subtract, ALU.mult).then_inc(z_ready, 1)

            def rope(g):
                r, a = rope_index(g), attention_index(g)
                wait(dve, qk_done, a + 1)
                wait(dve, qk_summed, r - 1)
                for at, table, dst in ((0, C_COS, t1), (256, C_SIN, t2)):
                    i = nc.vector.tensor_tensor(dst[:, r % 2].rearrange("p a b s -> p (a b) s"),
                                                QK_ps[:, at:at + 256].rearrange("p (a s) -> p a s", s=S),
                                                const[:, table:table + S].unsqueeze(1).broadcast_to([128, 4, S]), ALU.mult)
                i.then_inc(roped, 1)

            def rest_parts(g):
                a = attention_index(g)
                wait(dve, high_ready, a + 1)
                wait(dve, qm_ready, 4 * (a - 1))
                wait(dve, k2_ready, a - 1)
                nc.vector.tensor_tensor(parts[:, a % 2, 1].rearrange("p n b s -> p (n b s)"),
                                        qkT[:, a % 2].rearrange("p n b s -> p (n b s)"),
                                        parts[:, a % 2, 0].bitcast(F32).rearrange("p n b s -> p (n b s)"),
                                        ALU.subtract).then_inc(rest_ready, 1)

            def row_maxima(g):
                a = attention_index(g)
                wait(dve, s_done, a + 1)
                wait(dve, mt_done, a - 1)
                nc.vector.tensor_reduce(m[:, a % 2], S_ps[:].rearrange("p (h k) -> p h k", k=S), AX.X,
                                        ALU.max).then_inc(max_done, 1)

            def spread_maxima(g):
                a = attention_index(g)
                wait(dve, mt_done, a + 1)
                wait(dve, st_done, a - 1)
                nc.vector.tensor_tensor(mexp[:, a % 2], T_ps[0:16, 256:384].unsqueeze(1).broadcast_to([16, 4, 128]),
                                        few[:, F_NEG:F_NEG + 4].unsqueeze(2).broadcast_to([16, 4, 128]),
                                        ALU.mult).then_inc(mexp_ready, 1)

            def invert_sums(g):
                a = attention_index(g)
                wait(dve, av_done, a + 1)
                wait(dve, rep_done, a - 1)
                nc.vector.reciprocal(rden[:, a % 2], O_ps[64:72, 0:256]).then_inc(rden_ready, 1)

            def divide(g):
                a = attention_index(g)
                wait(dve, rep_copied, a + 1)
                if a >= 2:
                    wait(dve, y_done, ATTN_ITEMS[a - 2] + 1)
                for G in range(2):
                    i = nc.vector.tensor_tensor(oT[64 * G:64 * G + 64, a % 2].rearrange("p b s -> p (b s)"),
                                                O_ps[0:64, 128 * G:128 * G + 128],
                                                rden_rows[:, a % 2, 128 * G:128 * G + 128], ALU.mult)
                i.then_inc(o_ready, 1)

            def add_residual(g):
                p = g % PAIRS
                wait(dve, y_done, g + 1)
                y = VY_ps[:, 256:384]
                if kind(g) in (SELF1, FFN1):
                    n = gated_before(g)
                    which = 0 if kind(g) == SELF1 else 1
                    nc.vector.tensor_tensor(gy[:, n % 2], y, gate_rep[:, p, which], ALU.mult).then_inc(gated, 1)
                    dve.wait_ge(gated, n + 1)
                    y = gy[:, n % 2]
                nc.vector.tensor_tensor(x[:, p], x[:, p], y, ALU.add).then_inc(x_ready, 1)

            for t in steps():
                if t == -1:
                    set_modulation()
                if t == GATES_STEP:
                    set_modulation_dit()
                    set_rows()
                    dve.wait_ge(rows_ready, 2)
                    for n in range(PAIRS // 2):
                        spread_gates(n)
                if attn(t - 3):
                    row_maxima(t - 3)
                if attn(t - 5):
                    divide(t - 5)
                if attn(t - 3):
                    spread_maxima(t - 3)
                if valid(t - 1) and kind(t - 1) in ROPE:
                    rope(t - 1)
                if valid(t + 1):
                    normalise(t + 1)
                if valid(t + 2):
                    statistics(t + 2)
                if attn(t - 1):
                    rest_parts(t - 1)
                if attn(t - 4):
                    invert_sums(t - 4)
                if valid(t - 5):
                    add_residual(t - 5)

        @block.tensor
        def _(pe):
            def matmul(out, lhsT, rhs, first=True, last=True):
                return nc.tensor.matmul(out, lhsT, rhs, start=first, stop=last)

            def modulation():
                pe.wait_ge(loaded["lnw"], 16)
                pe.wait_ge(loaded["vec"], 32)
                for k in range(6):
                    i = matmul(QK_ps[:, 16 * k:16 * k + 16], ln_w[:, 128 * k:128 * k + 128], condT[:])
                i.then_inc(mod_ps_done, 1)

            def modulation_dit():
                pe.wait_ge(loaded["mod"], 16)
                pe.wait_ge(silu_done, 1)
                pe.wait_ge(roped, 2 * PAIRS)
                for n, part in enumerate((0, 1, 3, 4)):
                    i = matmul(QK_ps[:, 96 + 16 * n:112 + 16 * n], wmod[:, 128 * part:128 * part + 128], siluT[:])
                i.then_inc(mod_ps_done, 1)

            def rows():
                ones = few[0:1, F_ONES:F_ONES + 128]
                pe.wait_ge(loaded["row"], 16)
                pe.wait_ge(o_ready, 2 * PAIRS)
                for n, (part, r) in enumerate(((2, R_GA), (5, R_GM))):
                    matmul(O_ps[0:16, 128 * n:128 * n + 128], siluT[:], wmod[:, 128 * part:128 * part + 128], last=False)
                    matmul(O_ps[0:16, 128 * n:128 * n + 128], ones[:, 0:16], row[:, r:r + 128], first=False)
                for n, (bv, o, r, part) in enumerate(((V_BV3, "o3", R_BP, 3), (V_BV4, "o4", R_BC, 4))):
                    pe.wait_ge(w_loaded[part], 16)
                    matmul(O_ps[0:1, 256 + 128 * n:384 + 128 * n], vec[:, bv:bv + 1], wt(o), last=False)
                    i = matmul(O_ps[0:1, 256 + 128 * n:384 + 128 * n], ones[:, 0:1], row[:, r:r + 128], first=False)
                i.then_inc(rows_ps_done, 1)

            def gates():
                pe.wait_ge(rows_ready, 2)
                for n in range(PAIRS // 2):
                    wait(pe, gate_ready, n)
                    for j in range(2):
                        p = 2 * n + j
                        i = matmul(O_ps[:, 256 * j:256 * j + 256],
                                   few[:, F_PAIR + 128 * p:F_PAIR + 128 * p + 128], gate[:])
                    i.then_inc(gate_ps_done, 1)

            def turn_input(g):
                wait(pe, z_ready, norms_before(g) + 1 + (kind(g) == CROSS1))
                wait(pe, xn_ready, g)
                wait(pe, mexp_ready, attn_upto(g - 4))
                n = 1 + (kind(g) == CROSS1)
                for i in range(n):
                    mm = nc.tensor.transpose(T_ps[:, 128 * i:128 * i + 128], z[:, g % 2, i], ident)
                mm.then_inc(t_done, 1)

            def turn_maxima(g):
                a = attention_index(g)
                wait(pe, max_done, a + 1)
                wait(pe, xn_ready, min(g + 4, N_ITEMS))
                nc.tensor.transpose(T_ps[0:16, 256:384], m[:, a % 2], ident).then_inc(mt_done, 1)

            def project(g):
                k, a, p = kind(g), attention_index(g), g % PAIRS
                pe.wait_ge(xn_ready, g + 1)
                if p == 0:
                    pe.wait_ge(w_loaded[k], 16)
                if g == CROSS0 * PAIRS:
                    pe.wait_ge(loaded["ctxT"], 16)
                if g == 0:
                    pe.wait_ge(mod_ready, 6)
                if g == SELF1 * PAIRS:
                    pe.wait_ge(mod_ready, 10)
                xin = xnT[:, g % 3, 0].rearrange("p b s -> p (b s)")
                kv = {SELF0: xin, SELF1: xin, CROSS0: ctxT[:, p].rearrange("p b s -> p (b s)"),
                      CROSS1: xnT[:, g % 3, 1].rearrange("p b s -> p (b s)")}[k]
                if k in ROPE:
                    wait(pe, roped, rope_index(g))
                else:
                    wait(pe, roped, 2 * PAIRS)
                    wait(pe, qk_copied, plain_index(g))
                parts = [("q", xin, 0), ("k", kv, 128)] + [("qs", xin, 256), ("ks", kv, 384)] * (k in ROPE)
                for name, rhs, at in parts:
                    i = matmul(QK_ps[:, at:at + 128], wt(f"{name}{k}"), rhs)
                i.then_inc(qk_done, 1)
                wait(pe, v_ready, a)
                wait(pe, x_ready, g - 4)
                for h2 in range(2):
                    for b in range(2):
                        i = matmul(VY_ps[64 * h2:64 * h2 + 64, 64 * b:64 * b + 64], kv[:, 64 * b:64 * b + 64],
                                   wt(f"v{k}")[:, 64 * h2:64 * h2 + 64])
                i.then_inc(v_done, 1)
                return i

            def scores_by_query(g):
                a = attention_index(g)
                wait(pe, qm_ready, 4 * (a + 1))
                wait(pe, k2_ready, a + 1)
                wait(pe, max_done, a)
                wait(pe, gelu_done, ffn_index(g))
                for b in range(2):
                    for j in range(4):
                        at = 512 * b + 128 * j
                        i = matmul(S_ps[:, at:at + 128], QM[:, a % 3, 0, b, 2 * j:2 * j + 2].rearrange("p h s -> p (h s)"),
                                   K2[:, a % 3, 0, b].rearrange("p h s -> p (h s)"))
                i.then_inc(s_done, 1)

            def scores_by_key(g):
                a = attention_index(g)
                wait(pe, mexp_ready, a + 1)
                wait(pe, p_ready, a)
                if a == 0:
                    pe.wait_ge(sel_ready, 1)
                for b in range(2):
                    out = ST_ps[:, 512 * b:512 * b + 512]
                    for n, (k_part, q_part) in enumerate(((0, 1), (1, 0), (0, 0))):
                        matmul(out, K2[:, a % 3, k_part, b].rearrange("p h s -> p (h s)"),
                               QM[:, a % 3, q_part, b].rearrange("p h s -> p (h s)"), n == 0, False)
                    i = matmul(out, sel[:, b], mexp[:, a % 2].rearrange("p j s -> p (j s)"), first=False)
                i.then_inc(st_done, 1)

            def weigh_values(g):
                a = attention_index(g)
                wait(pe, p_ready, a + 1)
                wait(pe, v_ready, a + 1)
                wait(pe, o_ready, a)
                if g == SELF1 * PAIRS:
                    pe.wait_ge(gate_ready, PAIRS // 2)
                for G in range(2):
                    for b in range(2):
                        out = O_ps[0:72, 128 * G + 64 * b:128 * G + 64 * b + 64]
                        for hp4 in range(4):
                            hp = 4 * G + hp4
                            i = matmul(out, VM[:, a % 4, b, hp], P[:, a % 2, b, hp], hp4 == 0, hp4 == 3)
                i.then_inc(av_done, 1)

            def spread_sums(g):
                a = attention_index(g)
                wait(pe, rden_ready, a + 1)
                matmul(O_ps[0:64, 256:512], few[0:8, F_REP:F_REP + 64], rden[:, a % 2]).then_inc(rep_done, 1)

            def first_product(g):
                n = ffn_index(g)
                pe.wait_ge(xn_ready, g + 1)
                if g % PAIRS == 0:
                    pe.wait_ge(w_loaded[kind(g)], 16)
                wait(pe, max_done, attention_index(g))
                wait(pe, gelu_done, n)
                for c in range(FFC):
                    i = matmul(S_ps[:, 128 * c:128 * c + 128], wt(f"w1_{kind(g)}")[:, 128 * c:128 * c + 128],
                               xnT[:, g % 3, 0].rearrange("p b s -> p (b s)"))
                i.then_inc(h_done, 1)

            def block_output(g):
                k = kind(g)
                if g == FFN0 * PAIRS:
                    pe.wait_ge(loaded["row"], 16)
                y = VY_ps[:, 256:384]
                wait(pe, v_ready, attn_upto(g + 4))
                wait(pe, x_ready, g)
                if k in ATTN:
                    a = attention_index(g)
                    wait(pe, o_ready, a + 1)
                    i = matmul(y, oT[:, a % 2].rearrange("p b s -> p (b s)"), wt(f"o{k}"), last=k in ROPE)
                    bias = {SELF1: brow[:, 0], CROSS1: brow[:, 1]}.get(k)
                else:
                    n = ffn_index(g)
                    wait(pe, gelu_done, n + 1)
                    for c in range(FFC):
                        matmul(y, hT[:, n % 3, c], wt(f"w2_{k}")[:, 128 * c:128 * c + 128], c == 0, False)
                    r = R_FB2 if k == FFN0 else R_MB2
                    bias = row[:, r:r + 128]
                if bias is not None:
                    i = matmul(y, few[0:1, F_ONES:F_ONES + 128], bias, first=False)
                i.then_inc(y_done, 1)

            modulation()
            for t in steps():
                if t == GATES_STEP:
                    modulation_dit()
                    rows()
                    gates()
                if valid(t):
                    if t == 0:
                        pe.wait_ge(loaded["const"], 16)
                    turn_input(t)
                if attn(t - 1):
                    project(t - 1)
                if attn(t - 3):
                    turn_maxima(t - 3)
                if attn(t - 4):
                    weigh_values(t - 4)
                if valid(t - 5):
                    block_output(t - 5)
                if attn(t - 3):
                    scores_by_key(t - 3)
                if attn(t - 2):
                    scores_by_query(t - 2)
                if ffn(t - 2):
                    first_product(t - 2)
                if attn(t - 4):
                    spread_sums(t - 4)


def _packed_weights(i):
    def swapped(wt):
        return wt.reshape(D, H, 2, HD // 2)[:, :, ::-1].reshape(D, D)

    def by_tiles(wt):
        return wt.reshape(2, 2, 4, HD, -1).transpose(1, 0, 2, 3, 4).reshape(D, -1)

    def chunks(wt):
        return wt.reshape(FFC, 128, D).transpose(1, 0, 2).reshape(128, FFC * D)

    def L0(name):
        return i["L0_xcond_" + name].T

    def L1(name):
        return i["L1_xcond_" + name]

    blocks = {"v0": L0("qkv_w")[:, 256:], "o0": by_tiles(L0("sa_out_w")), "v1": L0("v_w"), "o1": by_tiles(L0("ca_out_w")),
              "w1_2": L0("ffn_w1"), "w2_2": chunks(L0("ffn_w2")),
              "q3": L1("W_qkv")[:, :128], "k3": L1("W_qkv")[:, 128:256], "v3": L1("W_qkv")[:, 256:],
              "o3": by_tiles(L1("W_proj")), "q4": L1("W_qc"), "k4": L1("W_kvc")[:, :128], "v4": L1("W_kvc")[:, 128:],
              "o4": by_tiles(L1("W_cproj")), "w1_5": L1("W_mlp1"), "w2_5": chunks(L1("W_mlp2"))}
    for n, (q, k) in enumerate(((L0("qkv_w")[:, :128], L0("qkv_w")[:, 128:256]), (L0("q_w"), L0("k_w")))):
        blocks.update({f"q{n}": q, f"k{n}": k, f"qs{n}": swapped(q), f"ks{n}": swapped(k)})
    return np.concatenate([blocks[name] for name in W_COLS], axis=1)


def _packed_vectors(i):
    def by_tiles(v):
        return v.reshape(2, 2, 4, HD).transpose(1, 0, 2, 3).reshape(D)

    cols = []
    for n in (1, 2, 3):
        cols += list(i[f"L0_xcond_ln{n}_b"].reshape(2, D))
    cols += list(i["L1_xcond_b_mod"].reshape(6, D))
    cols += list(i["L0_xcond_ffn_b1"].reshape(FFC, 128))
    cols += list(i["L1_xcond_b_mlp1"].reshape(FFC, 128))
    qkv, kv = i["L1_xcond_b_qkv"].reshape(3, D), i["L1_xcond_b_kvc"].reshape(2, D)
    cols += [qkv[0], qkv[1], i["L1_xcond_b_qc"], kv[0], by_tiles(qkv[2]), by_tiles(kv[1])]
    mod = i["L1_xcond_b_mod"].reshape(6, D)
    rows = [i["L0_xcond_ffn_b2"], i["L1_xcond_b_proj"], i["L1_xcond_b_cproj"], i["L1_xcond_b_mlp2"], mod[2], mod[5]]
    return np.stack(cols, axis=1), np.concatenate(rows)[None, :]


def kernel(**inputs):
    import concourse.bacc as bacc
    from concourse.bass_utils import run_bass_kernel_spmd

    i = {k: np.asarray(v) for k, v in inputs.items()}
    vec, row = _packed_vectors(i)
    ctx = i["ctx_1024"].reshape(B * S, D)
    arrays = {
        "x": i["x"].reshape(B * S, D),
        "ctx": ctx,
        "ctxT": ctx.T.reshape(D, PAIRS, 2, S),
        "condT": i["cond_1024"].T,
        "w": _packed_weights(i),
        "lnw": np.concatenate([i[f"L0_xcond_ln{n}_w"].T for n in (1, 2, 3)], axis=1),
        "wmod": i["L1_xcond_W_mod"],
        "vec": vec,
        "row": row,
        "const": _constants()[0],
        "few": _constants()[1],
    }
    nc = bacc.Bacc("TRN2", target_bir_lowering=False, num_devices=1)
    ins, args = {}, []
    for name, a in arrays.items():
        ins[f"in_{name}"] = np.ascontiguousarray(a)
        args.append(nc.dram_tensor(f"in_{name}", a.shape, F32, kind="ExternalInput").ap())
    args.append(nc.dram_tensor("out_x", (B * S, D), F32, kind="ExternalOutput").ap())
    build(nc, *args)
    r = run_bass_kernel_spmd(nc, [ins], core_ids=[0])
    return r.results[0]["out_x"].reshape(B, S, D)
```

```python
from contextlib import ExitStack

import numpy as np

import concourse.bass as bass
from concourse import mybir

F32 = mybir.dt.float32
F32R = mybir.dt.float32r
ALU = mybir.AluOpType
ACT = mybir.ActivationFunctionType
AX = mybir.AxisListType

B, S, D = 16, 64, 128
H, HD = 16, 8
FF = 512
PAIRS = B // 2
FFC = FF // 128
SCALE = HD ** -0.5
EPS = {0: 1e-5, 1: 1e-6}

SELF0, CROSS0, FFN0, SELF1, CROSS1, FFN1 = range(6)
KINDS = [SELF0, CROSS0, FFN0, SELF1, CROSS1, FFN1]
LAYER = {SELF0: 0, CROSS0: 0, FFN0: 0, SELF1: 1, CROSS1: 1, FFN1: 1}
ATTN = (SELF0, CROSS0, SELF1, CROSS1)
ROPE = (SELF0, CROSS0)
N_ITEMS = len(KINDS) * PAIRS
DIT_STEP = 0
LAST_LAG = 5

W_COLS = {}


def _w_columns():
    at = 0
    for name, n in (("q0", 128), ("k0", 128), ("qs0", 128), ("ks0", 128), ("v0", 128), ("o0", 128),
                    ("q1", 128), ("k1", 128), ("qs1", 128), ("ks1", 128), ("v1", 128), ("o1", 128),
                    ("w1_2", FF), ("w2_2", FF),
                    ("q3", 128), ("k3", 128), ("v3", 128), ("o3", 128),
                    ("q4", 128), ("k4", 128), ("v4", 128), ("o4", 128),
                    ("w1_5", FF), ("w2_5", FF)):
        W_COLS[name] = (at, at + n)
        at += n
    return at


W_N = _w_columns()
W_PARTS = [(0, W_COLS["o0"][1]), (W_COLS["q1"][0], W_COLS["o1"][1]), (W_COLS["w1_2"][0], W_COLS["w2_2"][1]),
           (W_COLS["q3"][0], W_COLS["o3"][1]), (W_COLS["q4"][0], W_COLS["o4"][1]),
           (W_COLS["w1_5"][0], W_COLS["w2_5"][1])]

V_LN = 0
V_MOD = 6
V_FB1 = 12
V_MB1 = 16
V_Q3, V_K3, V_Q4, V_K4 = 20, 21, 22, 23
V_BV3, V_BV4 = 24, 25
V_N = 26
R_FB2, R_BP, R_BC, R_MB2, R_GA, R_GM, R_N = 0, 128, 256, 384, 512, 640, 768

C_ID, C_COS, C_SIN, C_HP, C_N = 0, 128, 192, 256, 264
F_NEG, F_SEL, F_PAIR, F_ONES, F_N = 0, 4, 260, 1284, 1412
VC = HD + 1


def _constants():
    c = np.zeros((128, C_N), np.float32)
    f = np.zeros((16, F_N), np.float32)
    c[:, C_ID:C_ID + 128] = np.eye(128, dtype=np.float32)
    half = HD // 2
    inv_freq = (np.float32(1.0) / np.power(np.float32(10000.0), np.arange(half, dtype=np.float32) / half)).astype(np.float32)
    ang = np.arange(S, dtype=np.float32)[:, None] * inv_freq[None, :]
    p = np.arange(128)
    c[:, C_COS:C_COS + S] = np.cos(ang).astype(np.float32).T[p % half]
    sign = np.where(p % HD < half, np.float32(-1), np.float32(1))[:, None]
    c[:, C_SIN:C_SIN + S] = sign * np.sin(ang).astype(np.float32).T[p % half]
    c[p, C_HP + (p // HD) % 8] = 1.0
    for b in range(2):
        for j in range(4):
            for h2 in range(2):
                r = b * 8 + j * 2 + h2
                f[r, F_NEG + j] = -1.0
                f[r, F_SEL + b * 128 + h2 * 64:F_SEL + b * 128 + h2 * 64 + 64] = 1.0
    for b in range(B):
        f[b, F_PAIR + b * S:F_PAIR + (b + 1) * S] = 1.0
    f[:, F_ONES:] = 1.0
    return c, f


def attention_index(g):
    block, pair = divmod(g, PAIRS)
    return sum(k in ATTN for k in KINDS[:block]) * PAIRS + (pair if KINDS[block] in ATTN else 0)


def ffn_index(g):
    block, pair = divmod(g, PAIRS)
    return sum(k not in ATTN for k in KINDS[:block]) * PAIRS + (pair if KINDS[block] not in ATTN else 0)


def plain_index(g):
    block, pair = divmod(g, PAIRS)
    return sum(k in (SELF1, CROSS1) for k in KINDS[:block]) * PAIRS + (pair if KINDS[block] in (SELF1, CROSS1) else 0)


def rope_index(g):
    block, pair = divmod(g, PAIRS)
    return sum(k in ROPE for k in KINDS[:block]) * PAIRS + (pair if KINDS[block] in ROPE else 0)


ATTN_ITEMS = [g for g in range(N_ITEMS) if KINDS[g // PAIRS] in ATTN]
FFN_ITEMS = [g for g in range(N_ITEMS) if KINDS[g // PAIRS] not in ATTN]


def build(nc, x_d, ctx_d, ctxT_d, condT_d, w_d, lnw_d, wmod_d, vec_d, row_d, const_d, few_d, out_d):
    with ExitStack() as stack:
        def sb(name, shape, dt=F32):
            return stack.enter_context(nc.sbuf_tensor(name, shape, dt))

        def ps(name, shape):
            return stack.enter_context(nc.psum_tensor(name, shape, F32))

        def sem(name):
            return stack.enter_context(nc.semaphore(name))

        x = sb("x", [128, PAIRS, D])
        ctx = sb("ctx", [128, PAIRS, D])
        ctxT = sb("ctxT", [D, PAIRS, 2, S])
        w = sb("w", [128, W_N])
        wmod = sb("wmod", [D, 6 * D])
        ln_w = sb("ln_w", [D, 6 * D])
        vec = sb("vec", [D, V_N])
        row = sb("row", [1, R_N])
        const = sb("const", [128, C_N])
        few = sb("few", [16, F_N])
        condT = sb("condT", [D, B])
        sel = sb("sel", [16, 2, 128], F32R)
        mod_scale = sb("mod_scale", [D, 5, B])
        mod_shift = sb("mod_shift", [D, 5, B])
        siluT = sb("siluT", [D, B])
        gate = sb("gate", [B, 2, 2 * D], F32R)
        pairs = sb("pairs", [B, PAIRS * 2 * S], F32R)
        gate_rep = sb("gate_rep", [128, PAIRS, 2, D])
        brow = sb("brow", [1, 2, D])
        stats = sb("stats", [128, 2, 2, 6])
        mv = sb("mv", [128, 2, 2, 2])
        var = sb("var", [128, 2, 2])
        rstd = sb("rstd", [128, 2, 2])
        minus_half = sb("minus_half", [128, 1])
        z = sb("z", [128, 2, 2, D])
        xnT = sb("xnT", [D, 3, 2, 2, S])
        t1 = sb("t1", [128, 2, 2, 2, S])
        t2 = sb("t2", [128, 2, 2, 2, S])
        qkT = sb("qkT", [128, 2, 2, 2, S])
        parts = sb("parts", [128, 2, 2, 2, 2, S], F32R)
        QM = sb("QM", [128, 3, 2, 2, 8, S], F32R)
        K2 = sb("K2", [128, 3, 2, 2, 2, S], F32R)
        VM = sb("VM", [128, 4, 2, 8, 2 * VC])
        m = sb("m", [128, 2, 16])
        mexp = sb("mexp", [16, 2, 4, 128], F32R)
        P = sb("P", [128, 2, 2, 8, S])
        rden = sb("rden", [128, 2, H])
        o = sb("o", [128, 2, D])
        oT = sb("oT", [128, 2, 2, S])
        hT = sb("hT", [128, 3, FFC, 128])
        gy = sb("gy", [128, 2, D])
        T_ps = ps("T_ps", [128, 512])
        QK_ps = ps("QK_ps", [128, 512])
        VY_ps = ps("VY_ps", [128, 512])
        O_ps = ps("O_ps", [128, 512])
        S_ps = ps("S_ps", [128, 1024])
        ST_ps = ps("ST_ps", [128, 1024])

        ident = const[:, C_ID:C_ID + 128]

        loaded = {n: sem(f"loaded_{n}") for n in ("x0", "x", "ctx", "ctxT", "const", "few", "vec", "lnw", "mod", "row")}
        w_loaded = [sem(f"w_loaded_{n}") for n in range(len(W_PARTS))]
        zeroed = sem("zeroed")
        den_set = sem("den_set")
        silu_done = sem("silu_done")
        mod_ps_done = sem("mod_ps_done")
        mod_ready = sem("mod_ready")
        rows_ps_done = sem("rows_ps_done")
        rows_ready = sem("rows_ready")
        pairs_ready = sem("pairs_ready")
        gate_ps_done = sem("gate_ps_done")
        gate_ready = sem("gate_ready")
        sel_ready = sem("sel_ready")
        stats_done = sem("stats_done")
        mv_done = sem("mv_done")
        var_done = sem("var_done")
        rstd_done = sem("rstd_done")
        z_ready = sem("z_ready")
        t_done = sem("t_done")
        xn_ready = sem("xn_ready")
        qk_done = sem("qk_done")
        v_done = sem("v_done")
        roped = sem("roped")
        qk_summed = sem("qk_summed")
        qk_copied = sem("qk_copied")
        high_ready = sem("high_ready")
        rest_ready = sem("rest_ready")
        k2_ready = sem("k2_ready")
        qm_ready = sem("qm_ready")
        rest_spread = sem("rest_spread")
        v_ready = sem("v_ready")
        s_done = sem("s_done")
        max_done = sem("max_done")
        mt_done = sem("mt_done")
        mexp_ready = sem("mexp_ready")
        st_done = sem("st_done")
        p_ready = sem("p_ready")
        av_done = sem("av_done")
        rden_ready = sem("rden_ready")
        o_divided = sem("o_divided")
        o_turned = sem("o_turned")
        o_ready = sem("o_ready")
        h_done = sem("h_done")
        gelu_done = sem("gelu_done")
        y_done = sem("y_done")
        gated = sem("gated")
        x_ready = sem("x_ready")
        stored = sem("stored")

        def wt(name):
            a, b = W_COLS[name]
            return w[:, a:b]

        def kind(g):
            return KINDS[g // PAIRS]

        def steps():
            return range(-2, N_ITEMS + LAST_LAG)

        def valid(g):
            return 0 <= g < N_ITEMS

        def attn(g):
            return valid(g) and kind(g) in ATTN

        def ffn(g):
            return valid(g) and kind(g) not in ATTN

        def wait(eng, signal, count):
            if count > 0:
                eng.wait_ge(signal, count)

        MODS = {SELF0: 0, CROSS0: 1, FFN0: 2, SELF1: 3, FFN1: 4}

        def gated_before(g):
            block, pair = divmod(g, PAIRS)
            return sum(k in (SELF1, FFN1) for k in KINDS[:block]) * PAIRS + (pair if KINDS[block] in (SELF1, FFN1) else 0)

        def norms_before(g):
            return g + min(max(g - CROSS1 * PAIRS, 0), PAIRS)

        block = stack.enter_context(nc.Block())

        @block.sync
        def _(sp):
            x_v = x_d.rearrange("(p t) d -> t p d", p=PAIRS)
            sp.dma_start(x[:, 0:1], x_v[:, 0:1]).then_inc(loaded["x0"], 16)
            sp.dma_start(ln_w[:], lnw_d).then_inc(loaded["lnw"], 16)
            sp.dma_start(x[:, 1:PAIRS], x_v[:, 1:PAIRS]).then_inc(loaded["x"], 16)
            for n in range(len(W_PARTS)):
                a, b = W_PARTS[n]
                sp.dma_start(w[:, a:b], w_d[:, a:b]).then_inc(w_loaded[n], 16)
                if n == 0:
                    sp.dma_start(wmod[:], wmod_d).then_inc(loaded["mod"], 16)
                if n == 1:
                    sp.dma_start(ctxT[:], ctxT_d).then_inc(loaded["ctxT"], 16)
            sp.dma_start(ctx[:], ctx_d.rearrange("(p t) d -> t p d", p=PAIRS)).then_inc(loaded["ctx"], 16)
            out_v = out_d.rearrange("(p t) d -> p t d", p=PAIRS)
            for p in range(PAIRS):
                sp.wait_ge(x_ready, (len(KINDS) - 1) * PAIRS + p + 1)
                sp.dma_start(out_v[p], x[:, p, :]).then_inc(stored, 16)
            sp.wait_ge(stored, 16 * PAIRS)

        @block.gpsimd
        def _(pool):
            nc.gpsimd.memset(K2[:].bitcast(F32), 0.0).then_inc(zeroed, 1)
            nc.gpsimd.memset(VM[:], 0.0).then_inc(zeroed, 1)
            nc.gpsimd.memset(minus_half[:], -0.5).then_inc(zeroed, 1)
            pool.wait_ge(zeroed, 3)
            for h2 in range(2):
                nc.gpsimd.memset(VM[64 * h2:64 * h2 + 64, :, :, :, VC * h2 + HD:VC * h2 + VC], 1.0).then_inc(den_set, 1)
            pool.wait_ge(den_set, 2)

            hp_mask = const[:, C_HP:C_HP + 8].unsqueeze(2).broadcast_to([128, 8, S])

            def spread_q(g):
                a = attention_index(g)
                if a == 0:
                    pool.wait_ge(loaded["const"], 16)
                wait(pool, st_done, a - 2)
                for part, b in ((0, 0), (0, 1), (1, 0)):
                    wait(pool, rest_ready if part else high_ready, a + 1)
                    q = parts[:, a % 2, part, 0, b, :].bitcast(F32).unsqueeze(1).broadcast_to([128, 8, S])
                    nc.gpsimd.tensor_tensor(QM[:, a % 3, part, b], q, hp_mask, ALU.mult).then_inc(qm_ready, 1)

            def invert_deviation(g):
                before = norms_before(g)
                if g >= 2:
                    wait(pool, z_ready, norms_before(g - 1))
                for i in range(1 + (kind(g) == CROSS1)):
                    wait(pool, var_done, before + i + 1)
                    nc.gpsimd.tensor_tensor(rstd[:, g % 2, i:i + 1], var[:, g % 2, i:i + 1], minus_half[:],
                                            ALU.pow).then_inc(rstd_done, 1)

            for t in steps():
                if attn(t - 2):
                    spread_q(t - 2)
                if valid(t + 1):
                    invert_deviation(t + 1)

        @block.scalar
        def _(act):
            act.dma_start(condT[:], condT_d).then_inc(loaded["vec"], 16)
            act.dma_start(vec[:], vec_d).then_inc(loaded["vec"], 16)
            act.dma_start(const[:], const_d).then_inc(loaded["const"], 16)
            act.dma_start(few[:], few_d).then_inc(loaded["few"], 16)
            act.dma_start(row[:], row_d).then_inc(loaded["row"], 16)
            act.wait_ge(loaded["vec"], 32)
            nc.scalar.activation(siluT[:], condT[:], ACT.Silu).then_inc(silu_done, 1)
            act.wait_ge(loaded["few"], 16)
            nc.scalar.activation(sel[:].rearrange("p b s -> p (b s)"), few[:, F_SEL:F_SEL + 256],
                                 ACT.Identity).then_inc(sel_ready, 1)
            nc.scalar.activation(pairs[:], few[:, F_PAIR:F_PAIR + PAIRS * 2 * S], ACT.Identity).then_inc(pairs_ready, 1)

            def modulate(g):
                p = g % PAIRS
                wait(act, t_done, g + 1)
                if attn(g - 3):
                    wait(act, v_done, attention_index(g - 3) + 1)
                if ffn(g - 3):
                    wait(act, h_done, ffn_index(g - 3) + 1)
                if kind(g) == CROSS1:
                    nc.scalar.activation(xnT[:, g % 3].rearrange("p c b s -> p (c b s)"), T_ps[:, 0:256],
                                         ACT.Identity).then_inc(xn_ready, 1)
                    return
                if g == 0:
                    act.wait_ge(mod_ready, 6)
                if g == SELF1 * PAIRS:
                    act.wait_ge(mod_ready, 10)
                k = MODS[kind(g)]
                for b in range(2):
                    i = nc.scalar.activation(xnT[:, g % 3, 0, b], T_ps[:, S * b:S * b + S], ACT.Identity,
                                             scale=mod_scale[:, k, 2 * p + b:2 * p + b + 1],
                                             bias=mod_shift[:, k, 2 * p + b:2 * p + b + 1])
                i.then_inc(xn_ready, 1)

            def add_qk_bias(g):
                a = attention_index(g)
                wait(act, qk_done, a + 1)
                wait(act, rest_ready, a - 1)
                for n, bias in enumerate({SELF1: (V_Q3, V_K3), CROSS1: (V_Q4, V_K4)}[kind(g)]):
                    i = nc.scalar.activation(qkT[:, a % 2, n].rearrange("p b s -> p (b s)"),
                                             QK_ps[:, 128 * n:128 * n + 128], ACT.Identity, bias=vec[:, bias:bias + 1])
                i.then_inc(qk_copied, 1)

            def high_parts(g):
                a = attention_index(g)
                if kind(g) in ROPE:
                    wait(act, qk_summed, rope_index(g) + 1)
                else:
                    wait(act, qk_copied, plain_index(g) + 1)
                wait(act, qm_ready, 3 * (a - 1))
                wait(act, k2_ready, a - 1)
                nc.scalar.activation(parts[:, a % 2, 0].rearrange("p n b s -> p (n b s)"),
                                     qkT[:, a % 2].rearrange("p n b s -> p (n b s)"), ACT.Identity).then_inc(high_ready, 1)

            def place_k(g):
                a = attention_index(g)
                if a == 0:
                    act.wait_ge(zeroed, 3)
                wait(act, rest_ready, a + 1)
                wait(act, st_done, a - 2)
                for h2 in range(2):
                    half = slice(64 * h2, 64 * h2 + 64)
                    i = nc.scalar.activation(K2[half, a % 3, :, :, h2, :], parts[half, a % 2, :, 1].bitcast(F32),
                                             ACT.Identity)
                i.then_inc(k2_ready, 1)

            def place_v(g):
                a = attention_index(g)
                if a == 0:
                    act.wait_ge(den_set, 2)
                wait(act, v_done, a + 1)
                wait(act, av_done, a - 3)
                for h2 in range(2):
                    for b in range(2):
                        i = nc.scalar.activation(VM[64 * h2:64 * h2 + 64, a % 4, b, :, VC * h2:VC * h2 + HD],
                                                 VY_ps[64 * b:64 * b + 64, 64 * h2:64 * h2 + 64].rearrange(
                                                     "p (h d) -> p h d", d=HD), ACT.Identity)
                i.then_inc(v_ready, 1)

            def exponentials(g):
                a = attention_index(g)
                wait(act, st_done, a + 1)
                wait(act, av_done, a - 1)
                nc.scalar.activation(P[:, a % 2].rearrange("p b h s -> p (b h s)"), ST_ps[:], ACT.Exp,
                                     scale=SCALE).then_inc(p_ready, 1)

            def copy_output(g):
                a = attention_index(g)
                wait(act, o_turned, a + 1)
                if a >= 2:
                    wait(act, y_done, ATTN_ITEMS[a - 2] + 1)
                nc.scalar.activation(oT[:, a % 2].rearrange("p b s -> p (b s)"), O_ps[:, 384:512],
                                     ACT.Identity).then_inc(o_ready, 1)

            def gelu(g):
                n = ffn_index(g)
                func, at = ((ACT.Gelu, V_FB1) if kind(g) == FFN0 else (ACT.Gelu_apprx_tanh, V_MB1))
                wait(act, h_done, n + 1)
                if n >= 3:
                    wait(act, y_done, FFN_ITEMS[n - 3] + 1)
                for c in range(FFC):
                    i = nc.scalar.activation(hT[:, n % 3, c], S_ps[:, 128 * c:128 * c + 128], func,
                                             bias=vec[:, at + c:at + c + 1])
                i.then_inc(gelu_done, 1)

            for t in steps():
                if valid(t):
                    modulate(t)
                if attn(t - 1) and kind(t - 1) not in ROPE:
                    add_qk_bias(t - 1)
                if attn(t - 1):
                    place_v(t - 1)
                    high_parts(t - 1)
                    place_k(t - 1)
                if attn(t - 3):
                    exponentials(t - 3)
                if attn(t - 4):
                    copy_output(t - 4)
                if ffn(t - 2):
                    gelu(t - 2)

        @block.vector
        def _(dve):
            def set_modulation():
                dve.wait_ge(mod_ps_done, 1)
                dve.wait_ge(loaded["vec"], 32)
                for k in range(3):
                    nc.vector.tensor_scalar(mod_scale[:, k], QK_ps[:, 32 * k:32 * k + 16], vec[:, 2 * k:2 * k + 1],
                                            1.0, ALU.add, ALU.add).then_inc(mod_ready, 1)
                    nc.vector.tensor_scalar(mod_shift[:, k], QK_ps[:, 32 * k + 16:32 * k + 32], vec[:, 2 * k + 1:2 * k + 2],
                                            None, ALU.add).then_inc(mod_ready, 1)

            def set_modulation_dit():
                dve.wait_ge(mod_ps_done, 2)
                for k, part in ((3, 0), (4, 3)):
                    at = 32 * (k - 3)
                    nc.vector.tensor_scalar(mod_shift[:, k], ST_ps[:, at:at + 16], vec[:, V_MOD + part:V_MOD + part + 1],
                                            None, ALU.add).then_inc(mod_ready, 1)
                    nc.vector.tensor_scalar(mod_scale[:, k], ST_ps[:, at + 16:at + 32],
                                            vec[:, V_MOD + part + 1:V_MOD + part + 2],
                                            1.0, ALU.add, ALU.add).then_inc(mod_ready, 1)

            def set_rows():
                dve.wait_ge(rows_ps_done, 1)
                nc.vector.tensor_copy(gate[:, 0], O_ps[0:16, 0:256]).then_inc(rows_ready, 1)
                nc.vector.tensor_copy(brow[:].rearrange("p a d -> p (a d)"), O_ps[0:1, 256:512]).then_inc(rows_ready, 1)
                dve.wait_ge(rows_ready, 1)
                nc.vector.tensor_tensor(gate[:, 1], O_ps[0:16, 0:256], gate[:, 0].bitcast(F32),
                                        ALU.subtract).then_inc(rows_ready, 1)

            def spread_gates(n):
                dve.wait_ge(gate_ps_done, n + 1)
                nc.vector.tensor_copy(gate_rep[:, 4 * n:4 * n + 4].rearrange("p n a d -> p (n a d)"),
                                      ST_ps[:]).then_inc(gate_ready, 1)

            def sources(g):
                return [x] + [ctx] * (kind(g) == CROSS1)

            def statistics(g):
                p, before = g % PAIRS, norms_before(g)
                if g == 0:
                    dve.wait_ge(loaded["x0"], 16)
                if g == 1:
                    dve.wait_ge(loaded["x"], 16)
                if g == CROSS1 * PAIRS:
                    dve.wait_ge(loaded["ctx"], 16)
                wait(dve, x_ready, g - PAIRS + 1)
                if g >= 2:
                    wait(dve, z_ready, norms_before(g - 1))
                for i, src in enumerate(sources(g)):
                    nc.vector.bn_stats(stats[:, g % 2, i], src[:, p]).then_inc(stats_done, 1)
                for i, src in enumerate(sources(g)):
                    dve.wait_ge(stats_done, before + i + 1)
                    nc.vector.bn_aggr(mv[:, g % 2, i], stats[:, g % 2, i]).then_inc(mv_done, 1)
                for i, src in enumerate(sources(g)):
                    dve.wait_ge(mv_done, before + i + 1)
                    nc.vector.tensor_scalar(var[:, g % 2, i:i + 1], mv[:, g % 2, i, 1:2], EPS[LAYER[kind(g)]], None,
                                            ALU.add).then_inc(var_done, 1)

            def normalise(g):
                p, before = g % PAIRS, norms_before(g)
                wait(dve, t_done, g - 1)
                for i, src in enumerate(sources(g)):
                    dve.wait_ge(rstd_done, before + i + 1)
                    nc.vector.tensor_scalar(z[:, g % 2, i], src[:, p], mv[:, g % 2, i, 0:1], rstd[:, g % 2, i:i + 1],
                                            ALU.subtract, ALU.mult).then_inc(z_ready, 1)

            def rope(g):
                r, a = rope_index(g), attention_index(g)
                if a == 0:
                    dve.wait_ge(loaded["const"], 16)
                wait(dve, qk_done, a + 1)
                wait(dve, qk_summed, r - 1)
                for at, table, dst in ((0, C_COS, t1), (256, C_SIN, t2)):
                    i = nc.vector.tensor_tensor(dst[:, r % 2].rearrange("p a b s -> p (a b) s"),
                                                QK_ps[:, at:at + 256].rearrange("p (a s) -> p a s", s=S),
                                                const[:, table:table + S].unsqueeze(1).broadcast_to([128, 4, S]), ALU.mult)
                i.then_inc(roped, 1)

            def rope_sum(g):
                r, a = rope_index(g), attention_index(g)
                wait(dve, roped, r + 1)
                wait(dve, rest_ready, a - 1)
                nc.vector.tensor_tensor(qkT[:, a % 2], t1[:, r % 2], t2[:, r % 2], ALU.add).then_inc(qk_summed, 1)

            def rest_parts(g):
                a = attention_index(g)
                wait(dve, high_ready, a + 1)
                wait(dve, qm_ready, 3 * (a - 1))
                wait(dve, k2_ready, a - 1)
                nc.vector.tensor_tensor(parts[:, a % 2, 1].rearrange("p n b s -> p (n b s)"),
                                        qkT[:, a % 2].rearrange("p n b s -> p (n b s)"),
                                        parts[:, a % 2, 0].bitcast(F32).rearrange("p n b s -> p (n b s)"),
                                        ALU.subtract).then_inc(rest_ready, 1)

            def spread_rest(g):
                a = attention_index(g)
                wait(dve, rest_ready, a + 1)
                wait(dve, st_done, a - 2)
                nc.vector.tensor_tensor(QM[:, a % 3, 1, 1],
                                        parts[:, a % 2, 1, 0, 1, :].bitcast(F32).unsqueeze(1).broadcast_to([128, 8, S]),
                                        const[:, C_HP:C_HP + 8].unsqueeze(2).broadcast_to([128, 8, S]),
                                        ALU.mult).then_inc(rest_spread, 1)

            def row_maxima(g):
                a = attention_index(g)
                wait(dve, mt_done, a - 1)
                for b in range(2):
                    wait(dve, s_done, 2 * a + b + 1)
                    i = nc.vector.tensor_reduce(m[:, a % 2, 8 * b:8 * b + 8],
                                                S_ps[:, 512 * b:512 * b + 512].rearrange("p (h k) -> p h k", k=S),
                                                AX.X, ALU.max)
                i.then_inc(max_done, 1)

            def spread_maxima(g):
                a = attention_index(g)
                if a == 0:
                    dve.wait_ge(loaded["few"], 16)
                wait(dve, mt_done, a + 1)
                wait(dve, st_done, a - 1)
                nc.vector.tensor_tensor(mexp[:, a % 2], T_ps[0:16, 256:384].unsqueeze(1).broadcast_to([16, 4, 128]),
                                        few[:, F_NEG:F_NEG + 4].unsqueeze(2).broadcast_to([16, 4, 128]),
                                        ALU.mult).then_inc(mexp_ready, 1)

            def sums_and_values():
                tile = O_ps[:, 0:16 * VC].rearrange("p (h g c) -> p g h c", g=2, c=VC)
                return tile[:, :, :, HD], tile[:, :, :, 0:HD]

            def invert_sums(g):
                a = attention_index(g)
                wait(dve, av_done, a + 1)
                wait(dve, o_divided, a - 1)
                nc.vector.reciprocal(rden[:, a % 2].rearrange("p (g h) -> p g h", g=2),
                                     sums_and_values()[0]).then_inc(rden_ready, 1)

            def divide(g):
                a = attention_index(g)
                wait(dve, rden_ready, a + 1)
                wait(dve, o_turned, a - 1)
                nc.vector.tensor_tensor(o[:, a % 2].rearrange("p (g h c) -> p g h c", g=2, c=HD), sums_and_values()[1],
                                        rden[:, a % 2].rearrange("p (g h) -> p g h", g=2).unsqueeze(3)
                                        .broadcast_to([128, 2, 8, HD]), ALU.mult).then_inc(o_divided, 1)

            def add_residual(g):
                p = g % PAIRS
                wait(dve, y_done, g + 1)
                y = VY_ps[:, 256:384]
                if kind(g) in (SELF1, FFN1):
                    n = gated_before(g)
                    which = 0 if kind(g) == SELF1 else 1
                    nc.vector.tensor_tensor(gy[:, n % 2], y, gate_rep[:, p, which], ALU.mult).then_inc(gated, 1)
                    dve.wait_ge(gated, n + 1)
                    y = gy[:, n % 2]
                nc.vector.tensor_tensor(x[:, p], x[:, p], y, ALU.add).then_inc(x_ready, 1)

            for t in steps():
                if t == -1:
                    set_modulation()
                if t == DIT_STEP + 1:
                    set_modulation_dit()
                    set_rows()
                if t in (DIT_STEP + 2, DIT_STEP + 3):
                    spread_gates(t - DIT_STEP - 2)
                if attn(t - 3):
                    row_maxima(t - 3)
                    spread_rest(t - 3)
                    spread_maxima(t - 3)
                if attn(t - 1) and kind(t - 1) in ROPE:
                    rope(t - 1)
                if valid(t + 1):
                    normalise(t + 1)
                if attn(t - 1) and kind(t - 1) in ROPE:
                    rope_sum(t - 1)
                if valid(t + 2):
                    statistics(t + 2)
                if attn(t - 1):
                    rest_parts(t - 1)
                if valid(t - 5):
                    add_residual(t - 5)
                if attn(t - 4):
                    invert_sums(t - 4)
                    divide(t - 4)

        @block.tensor
        def _(pe):
            def matmul(out, lhsT, rhs, first=True, last=True):
                return nc.tensor.matmul(out, lhsT, rhs, start=first, stop=last)

            issued = {"inputs": 0, "maxima": 0, "values": 0, "outputs": 0}

            def modulation():
                pe.wait_ge(loaded["lnw"], 16)
                pe.wait_ge(loaded["vec"], 32)
                for k in range(6):
                    i = matmul(QK_ps[:, 16 * k:16 * k + 16], ln_w[:, 128 * k:128 * k + 128], condT[:])
                i.then_inc(mod_ps_done, 1)

            def modulation_dit():
                pe.wait_ge(loaded["mod"], 16)
                pe.wait_ge(silu_done, 1)
                for n, part in enumerate((0, 1, 3, 4)):
                    i = matmul(ST_ps[:, 16 * n:16 * n + 16], wmod[:, 128 * part:128 * part + 128], siluT[:])
                i.then_inc(mod_ps_done, 1)

            def rows():
                ones = few[0:1, F_ONES:F_ONES + 128]
                pe.wait_ge(loaded["row"], 16)
                for n, (part, r) in enumerate(((2, R_GA), (5, R_GM))):
                    matmul(O_ps[0:16, 128 * n:128 * n + 128], siluT[:], wmod[:, 128 * part:128 * part + 128], last=False)
                    matmul(O_ps[0:16, 128 * n:128 * n + 128], ones[:, 0:16], row[:, r:r + 128], first=False)
                for n, (bv, o, r, part) in enumerate(((V_BV3, "o3", R_BP, 3), (V_BV4, "o4", R_BC, 4))):
                    pe.wait_ge(w_loaded[part], 16)
                    matmul(O_ps[0:1, 256 + 128 * n:384 + 128 * n], vec[:, bv:bv + 1], wt(o), last=False)
                    i = matmul(O_ps[0:1, 256 + 128 * n:384 + 128 * n], ones[:, 0:1], row[:, r:r + 128], first=False)
                i.then_inc(rows_ps_done, 1)

            def gates(n):
                pe.wait_ge(rows_ready, 3)
                pe.wait_ge(pairs_ready, 1)
                pe.wait_ge(mod_ready, 10)
                wait(pe, gate_ready, n)
                for j in range(4):
                    p = 4 * n + j
                    for part in range(2):
                        i = matmul(ST_ps[:, 256 * j:256 * j + 256], pairs[:, 128 * p:128 * p + 128], gate[:, part],
                                   part == 0, part == 1)
                i.then_inc(gate_ps_done, 1)

            def turn_input(g):
                wait(pe, z_ready, norms_before(g) + 1 + (kind(g) == CROSS1))
                wait(pe, xn_ready, g)
                wait(pe, mexp_ready, issued["maxima"])
                issued["inputs"] += 1
                n = 1 + (kind(g) == CROSS1)
                for i in range(n):
                    mm = nc.tensor.transpose(T_ps[:, 128 * i:128 * i + 128], z[:, g % 2, i], ident)
                mm.then_inc(t_done, 1)

            def turn_maxima(g):
                a = attention_index(g)
                wait(pe, max_done, a + 1)
                wait(pe, mexp_ready, a)
                wait(pe, xn_ready, issued["inputs"])
                issued["maxima"] += 1
                nc.tensor.transpose(T_ps[0:16, 256:384], m[:, a % 2], ident).then_inc(mt_done, 1)

            def project(g):
                k, a, p = kind(g), attention_index(g), g % PAIRS
                pe.wait_ge(xn_ready, g + 1)
                if p == 0:
                    pe.wait_ge(w_loaded[k], 16)
                if g == CROSS0 * PAIRS:
                    pe.wait_ge(loaded["ctxT"], 16)
                if g == 0:
                    pe.wait_ge(mod_ready, 6)
                if g == SELF1 * PAIRS:
                    pe.wait_ge(mod_ready, 10)
                xin = xnT[:, g % 3, 0].rearrange("p b s -> p (b s)")
                kv = {SELF0: xin, SELF1: xin, CROSS0: ctxT[:, p].rearrange("p b s -> p (b s)"),
                      CROSS1: xnT[:, g % 3, 1].rearrange("p b s -> p (b s)")}[k]
                if k in ROPE:
                    wait(pe, roped, rope_index(g))
                else:
                    wait(pe, roped, 2 * PAIRS)
                    wait(pe, qk_copied, plain_index(g))
                parts = [("q", xin, 0), ("k", kv, 128)] + [("qs", xin, 256), ("ks", kv, 384)] * (k in ROPE)
                for name, rhs, at in parts:
                    i = matmul(QK_ps[:, at:at + 128], wt(f"{name}{k}"), rhs)
                i.then_inc(qk_done, 1)
                wait(pe, v_ready, a)
                wait(pe, x_ready, issued["outputs"])
                issued["values"] += 1
                i = matmul(VY_ps[:, 0:128], kv, wt(f"v{k}"))
                i.then_inc(v_done, 1)
                return i

            def scores_by_query(g):
                a = attention_index(g)
                wait(pe, qm_ready, 3 * (a + 1))
                wait(pe, k2_ready, a + 1)
                wait(pe, max_done, a)
                wait(pe, gelu_done, ffn_index(g))
                for b in range(2):
                    for j in range(4):
                        at = 512 * b + 128 * j
                        i = matmul(S_ps[:, at:at + 128], QM[:, a % 3, 0, b, 2 * j:2 * j + 2].rearrange("p h s -> p (h s)"),
                                   K2[:, a % 3, 0, b].rearrange("p h s -> p (h s)"))
                    i.then_inc(s_done, 1)

            def scores_by_key(g):
                a = attention_index(g)
                wait(pe, mexp_ready, a + 1)
                wait(pe, rest_spread, a + 1)
                wait(pe, p_ready, a)
                if a == 0:
                    pe.wait_ge(sel_ready, 1)
                    pe.wait_ge(gate_ready, 2)
                for b in range(2):
                    out = ST_ps[:, 512 * b:512 * b + 512]
                    for n, (k_part, q_part) in enumerate(((0, 1), (1, 0), (0, 0))):
                        matmul(out, K2[:, a % 3, k_part, b].rearrange("p h s -> p (h s)"),
                               QM[:, a % 3, q_part, b].rearrange("p h s -> p (h s)"), n == 0, False)
                    i = matmul(out, sel[:, b], mexp[:, a % 2].rearrange("p j s -> p (j s)"), first=False)
                i.then_inc(st_done, 1)

            def weigh_values(g):
                a = attention_index(g)
                wait(pe, p_ready, a + 1)
                wait(pe, v_ready, a + 1)
                wait(pe, o_ready, a)
                if a == 0:
                    pe.wait_ge(rows_ready, 3)
                for b in range(2):
                    for hp in range(8):
                        at = 2 * VC * hp
                        i = matmul(O_ps[64 * b:64 * b + 64, at:at + 2 * VC], P[:, a % 2, b, hp], VM[:, a % 4, b, hp])
                i.then_inc(av_done, 1)

            def turn_output(g):
                a = attention_index(g)
                wait(pe, o_divided, a + 1)
                nc.tensor.transpose(O_ps[:, 384:512], o[:, a % 2], ident).then_inc(o_turned, 1)

            def first_product(g):
                n = ffn_index(g)
                pe.wait_ge(xn_ready, g + 1)
                if g % PAIRS == 0:
                    pe.wait_ge(w_loaded[kind(g)], 16)
                wait(pe, max_done, attention_index(g))
                wait(pe, gelu_done, n)
                for c in range(FFC):
                    i = matmul(S_ps[:, 128 * c:128 * c + 128], wt(f"w1_{kind(g)}")[:, 128 * c:128 * c + 128],
                               xnT[:, g % 3, 0].rearrange("p b s -> p (b s)"))
                i.then_inc(h_done, 1)

            def block_output(g):
                k = kind(g)
                if g == FFN0 * PAIRS:
                    pe.wait_ge(loaded["row"], 16)
                y = VY_ps[:, 256:384]
                wait(pe, v_ready, issued["values"])
                wait(pe, x_ready, g)
                issued["outputs"] += 1
                if k in ATTN:
                    a = attention_index(g)
                    wait(pe, o_ready, a + 1)
                    i = matmul(y, oT[:, a % 2].rearrange("p b s -> p (b s)"), wt(f"o{k}"), last=k in ROPE)
                    bias = {SELF1: brow[:, 0], CROSS1: brow[:, 1]}.get(k)
                else:
                    n = ffn_index(g)
                    wait(pe, gelu_done, n + 1)
                    for c in range(FFC):
                        matmul(y, hT[:, n % 3, c], wt(f"w2_{k}")[:, 128 * c:128 * c + 128], c == 0, False)
                    r = R_FB2 if k == FFN0 else R_MB2
                    bias = row[:, r:r + 128]
                if bias is not None:
                    i = matmul(y, few[0:1, F_ONES:F_ONES + 128], bias, first=False)
                i.then_inc(y_done, 1)

            modulation()
            for t in steps():
                if attn(t - 1):
                    project(t - 1)
                if attn(t - 3):
                    turn_maxima(t - 3)
                if attn(t - 4):
                    weigh_values(t - 4)
                if valid(t - 5):
                    block_output(t - 5)
                if attn(t - 3):
                    scores_by_key(t - 3)
                if attn(t - 2):
                    scores_by_query(t - 2)
                if ffn(t - 2):
                    first_product(t - 2)
                if attn(t - 4):
                    turn_output(t - 4)
                if valid(t + 1):
                    if t + 1 == 0:
                        pe.wait_ge(loaded["const"], 16)
                    turn_input(t + 1)
                if t == DIT_STEP:
                    modulation_dit()
                    rows()
                if t in (DIT_STEP + 1, DIT_STEP + 2):
                    gates(t - DIT_STEP - 1)


def _packed_weights(i):
    def swapped(wt):
        return wt.reshape(D, H, 2, HD // 2)[:, :, ::-1].reshape(D, D)

    def chunks(wt):
        return wt.reshape(FFC, 128, D).transpose(1, 0, 2).reshape(128, FFC * D)

    def L0(name):
        return i["L0_xcond_" + name].T

    def L1(name):
        return i["L1_xcond_" + name]

    blocks = {"v0": L0("qkv_w")[:, 256:], "o0": L0("sa_out_w"), "v1": L0("v_w"), "o1": L0("ca_out_w"),
              "w1_2": L0("ffn_w1"), "w2_2": chunks(L0("ffn_w2")),
              "q3": L1("W_qkv")[:, :128], "k3": L1("W_qkv")[:, 128:256], "v3": L1("W_qkv")[:, 256:],
              "o3": L1("W_proj"), "q4": L1("W_qc"), "k4": L1("W_kvc")[:, :128], "v4": L1("W_kvc")[:, 128:],
              "o4": L1("W_cproj"), "w1_5": L1("W_mlp1"), "w2_5": chunks(L1("W_mlp2"))}
    for n, (q, k) in enumerate(((L0("qkv_w")[:, :128], L0("qkv_w")[:, 128:256]), (L0("q_w"), L0("k_w")))):
        blocks.update({f"q{n}": q, f"k{n}": k, f"qs{n}": swapped(q), f"ks{n}": swapped(k)})
    return np.concatenate([blocks[name] for name in W_COLS], axis=1)


def _packed_vectors(i):
    cols = []
    for n in (1, 2, 3):
        cols += list(i[f"L0_xcond_ln{n}_b"].reshape(2, D))
    cols += list(i["L1_xcond_b_mod"].reshape(6, D))
    cols += list(i["L0_xcond_ffn_b1"].reshape(FFC, 128))
    cols += list(i["L1_xcond_b_mlp1"].reshape(FFC, 128))
    qkv, kv = i["L1_xcond_b_qkv"].reshape(3, D), i["L1_xcond_b_kvc"].reshape(2, D)
    cols += [qkv[0], qkv[1], i["L1_xcond_b_qc"], kv[0], qkv[2], kv[1]]
    mod = i["L1_xcond_b_mod"].reshape(6, D)
    rows = [i["L0_xcond_ffn_b2"], i["L1_xcond_b_proj"], i["L1_xcond_b_cproj"], i["L1_xcond_b_mlp2"], mod[2], mod[5]]
    return np.stack(cols, axis=1), np.concatenate(rows)[None, :]


def kernel(**inputs):
    import concourse.bacc as bacc
    from concourse.bass_utils import run_bass_kernel_spmd

    i = {k: np.asarray(v) for k, v in inputs.items()}
    vec, row = _packed_vectors(i)
    ctx = i["ctx_1024"].reshape(B * S, D)
    arrays = {
        "x": i["x"].reshape(B * S, D),
        "ctx": ctx,
        "ctxT": ctx.T.reshape(D, PAIRS, 2, S),
        "condT": i["cond_1024"].T,
        "w": _packed_weights(i),
        "lnw": np.concatenate([i[f"L0_xcond_ln{n}_w"].T for n in (1, 2, 3)], axis=1),
        "wmod": i["L1_xcond_W_mod"],
        "vec": vec,
        "row": row,
        "const": _constants()[0],
        "few": _constants()[1],
    }
    nc = bacc.Bacc("TRN2", target_bir_lowering=False, num_devices=1)
    ins, args = {}, []
    for name, a in arrays.items():
        ins[f"in_{name}"] = np.ascontiguousarray(a)
        args.append(nc.dram_tensor(f"in_{name}", a.shape, F32, kind="ExternalInput").ap())
    args.append(nc.dram_tensor("out_x", (B * S, D), F32, kind="ExternalOutput").ap())
    build(nc, *args)
    r = run_bass_kernel_spmd(nc, [ins], core_ids=[0])
    return r.results[0]["out_x"].reshape(B, S, D)
```
